# Optimizing a Trainium2 kernel written in Bass

```python
import numpy as np
import jax
import jax.numpy as jnp

def _softmax(x, axis=-1):
    return jax.nn.softmax(x, axis=axis)

def _gelu(x):
    return jax.nn.gelu(x, approximate=True)

def _silu(x):
    return jax.nn.silu(x)

def _sigmoid(x):
    return jax.nn.sigmoid(x)

def _layernorm(x, axis=-1, eps=1e-05):
    m = jnp.mean(x, axis=axis, keepdims=True)
    v = jnp.var(x, axis=axis, keepdims=True)
    return (x - m) / jnp.sqrt(v + eps)

def _scatter_add(tgt, idx, src, axis=0):
    return tgt.at[idx].add(src)

def _segment_sum(src, seg, n):
    return jax.ops.segment_sum(src, seg, n)
kernel_name = 'mk_adj_resnorm_d2_adj_r2_bc7989'

def setup_inputs(seed: int=0):
    np.random.seed(seed)
    _w = jnp.asarray

    def _rec_inputs():
        import jax
        import jax.numpy as jnp
        _gk = jax.random.key(seed)
        x = -0.0005207 + 1.001 * jax.random.normal(jax.random.fold_in(_gk, 1), (8, 1024, 128), jnp.float32)
        _a = jax.random.bernoulli(jax.random.fold_in(_gk, 2), 0.00195312, (1024, 1024))
        _a = jnp.logical_or(_a, jnp.swapaxes(_a, -1, -2))
        _a = jnp.logical_or(_a, jnp.eye(1024, dtype=bool))
        adj = _a.astype(jnp.int32)
        return (x, adj)
    x, adj = _rec_inputs()

    def _L0_gnn_setup():
        import jax, jax.numpy as jnp
        import numpy as np
        import math
        CHUNK = 128
        NUM_HEADS = 4
        EPS = 1e-05
        key = jax.random.key(seed)
        ks = jax.random.split(key, 12)
        B, N, F = (4, 1024, 128)
        x = jax.random.normal(ks[0], (B, N, F), dtype=jnp.float32)
        adj_matrix = jax.random.randint(ks[1], (N, N), 0, 2, dtype=jnp.int32)
        s = 1.0 / math.sqrt(F)
        Wq = jax.random.normal(ks[2], (F, F), dtype=jnp.float32) * s
        bq = jnp.zeros((F,), dtype=jnp.float32)
        Wk = jax.random.normal(ks[3], (F, F), dtype=jnp.float32) * s
        bk = jnp.zeros((F,), dtype=jnp.float32)
        Wv = jax.random.normal(ks[4], (F, F), dtype=jnp.float32) * s
        bv = jnp.zeros((F,), dtype=jnp.float32)
        Wo = jax.random.normal(ks[5], (F, F), dtype=jnp.float32) * s
        bo = jnp.zeros((F,), dtype=jnp.float32)
        gamma = jnp.ones((F,), dtype=jnp.float32)
        beta = jnp.zeros((F,), dtype=jnp.float32)
        return {'x': x, 'adj_matrix': adj_matrix, 'Wq': Wq, 'bq': bq, 'Wk': Wk, 'bk': bk, 'Wv': Wv, 'bv': bv, 'Wo': Wo, 'bo': bo, 'gamma': gamma, 'beta': beta}
    _L0_gnn_all = _L0_gnn_setup()
    _L0_gnn_in = {k: v for k, v in _L0_gnn_all.items() if k in ('Wq', 'bq', 'Wk', 'bk', 'Wv', 'bv', 'Wo', 'bo', 'gamma', 'beta')}
    del _L0_gnn_all

    def _L1_gnn_setup():
        import jax, jax.numpy as jnp
        import numpy as np
        B, N, D_IN, D_OUT, H = (64, 256, 128, 128, 4)
        HD = D_OUT // H
        key = jax.random.key(seed)
        ks = jax.random.split(key, 10)
        x = jax.random.normal(ks[0], (B, N, D_IN), dtype=jnp.float32)
        adj = jax.random.randint(ks[1], (N, N), 0, 2, dtype=jnp.int32)
        adj = adj.at[jnp.arange(N), jnp.arange(N)].set(1)
        s_in = 1.0 / np.sqrt(D_IN)
        s_out = 1.0 / np.sqrt(D_OUT)
        wq = jax.random.uniform(ks[2], (D_OUT, D_IN), jnp.float32, -s_in, s_in)
        bq = jax.random.uniform(ks[3], (D_OUT,), jnp.float32, -s_in, s_in)
        wk = jax.random.uniform(ks[4], (D_OUT, D_IN), jnp.float32, -s_in, s_in)
        bk = jax.random.uniform(ks[5], (D_OUT,), jnp.float32, -s_in, s_in)
        wv = jax.random.uniform(ks[6], (D_OUT, D_IN), jnp.float32, -s_in, s_in)
        bv = jax.random.uniform(ks[7], (D_OUT,), jnp.float32, -s_in, s_in)
        wo = jax.random.uniform(ks[8], (D_OUT, D_OUT), jnp.float32, -s_out, s_out)
        bo = jax.random.uniform(ks[9], (D_OUT,), jnp.float32, -s_out, s_out)
        return {'x': x, 'adj': adj, 'wq': wq, 'bq': bq, 'wk': wk, 'bk': bk, 'wv': wv, 'bv': bv, 'wo': wo, 'bo': bo}
    _L1_gnn_all = _L1_gnn_setup()
    _L1_gnn_in = {k: v for k, v in _L1_gnn_all.items() if k in ('wq', 'bq', 'wk', 'bk', 'wv', 'bv', 'wo', 'bo')}
    del _L1_gnn_all
    return {'x': x, 'adj': adj, 'L0_gnn_Wq': _L0_gnn_in['Wq'], 'L0_gnn_bq': _L0_gnn_in['bq'], 'L0_gnn_Wk': _L0_gnn_in['Wk'], 'L0_gnn_bk': _L0_gnn_in['bk'], 'L0_gnn_Wv': _L0_gnn_in['Wv'], 'L0_gnn_bv': _L0_gnn_in['bv'], 'L0_gnn_Wo': _L0_gnn_in['Wo'], 'L0_gnn_bo': _L0_gnn_in['bo'], 'L0_gnn_gamma': _L0_gnn_in['gamma'], 'L0_gnn_beta': _L0_gnn_in['beta'], 'L1_gnn_wq': _L1_gnn_in['wq'], 'L1_gnn_bq': _L1_gnn_in['bq'], 'L1_gnn_wk': _L1_gnn_in['wk'], 'L1_gnn_bk': _L1_gnn_in['bk'], 'L1_gnn_wv': _L1_gnn_in['wv'], 'L1_gnn_bv': _L1_gnn_in['bv'], 'L1_gnn_wo': _L1_gnn_in['wo'], 'L1_gnn_bo': _L1_gnn_in['bo']}

def reference(x, adj, L0_gnn_Wq, L0_gnn_bq, L0_gnn_Wk, L0_gnn_bk, L0_gnn_Wv, L0_gnn_bv, L0_gnn_Wo, L0_gnn_bo, L0_gnn_gamma, L0_gnn_beta, L1_gnn_wq, L1_gnn_bq, L1_gnn_wk, L1_gnn_bk, L1_gnn_wv, L1_gnn_bv, L1_gnn_wo, L1_gnn_bo):
    import jax
    import jax.numpy as jnp

    def _L0_gnn_ref(x, adj_matrix, Wq, bq, Wk, bk, Wv, bv, Wo, bo, gamma, beta):
        import jax, jax.numpy as jnp
        import numpy as np
        import math
        CHUNK = 128
        NUM_HEADS = 4
        EPS = 1e-05
        B, N, Fin = x.shape
        H = NUM_HEADS
        Dout = Wq.shape[0]
        Dh = Dout // H
        Nc = N // CHUNK
        q = (x @ Wq.T + bq).reshape(B, N, H, Dh).transpose(0, 2, 1, 3)
        k = (x @ Wk.T + bk).reshape(B, N, H, Dh).transpose(0, 2, 1, 3)
        v = (x @ Wv.T + bv).reshape(B, N, H, Dh).transpose(0, 2, 1, 3)
        kc = k.reshape(B, H, Nc, CHUNK, Dh)
        vc = v.reshape(B, H, Nc, CHUNK, Dh)
        scores = jnp.einsum('bhnd,bhjcd->bhnjc', q, kc) / jnp.sqrt(jnp.asarray(Dh, dtype=q.dtype))
        scores = jnp.clip(scores, -10.0, 10.0)
        mask = adj_matrix.reshape(N, Nc, CHUNK)[None, None]
        scores = jnp.where(mask == 0, jnp.asarray(-10.0, scores.dtype), scores)
        attn = jax.nn.softmax(scores, axis=-1)
        ctx = jnp.einsum('bhnjc,bhjcd->bhnd', attn, vc)
        ctx = ctx.transpose(0, 2, 1, 3).reshape(B, N, Dout)
        out = ctx @ Wo.T + bo
        out = out + x
        mu = jnp.mean(out, axis=-1, keepdims=True)
        var = jnp.mean(jnp.square(out - mu), axis=-1, keepdims=True)
        out = (out - mu) * jax.lax.rsqrt(var + EPS) * gamma + beta
        return out

    def _L1_gnn_ref(x, adj, wq, bq, wk, bk, wv, bv, wo, bo):
        import jax, jax.numpy as jnp
        import numpy as np
        B, N, D_IN, D_OUT, H = (64, 256, 128, 128, 4)
        HD = D_OUT // H
        b, n, _ = x.shape
        q = (x @ wq.T + bq).reshape(b, n, H, HD).transpose(0, 2, 1, 3)
        k = (x @ wk.T + bk).reshape(b, n, H, HD).transpose(0, 2, 1, 3)
        v = (x @ wv.T + bv).reshape(b, n, H, HD).transpose(0, 2, 1, 3)
        scores = jnp.einsum('bhnd,bhmd->bhnm', q, k) / jnp.sqrt(jnp.float32(HD))
        scores = jnp.where(adj[None, None] == 0, -jnp.inf, scores)
        attn = jnp.nan_to_num(jax.nn.softmax(scores, axis=-1), nan=0.0)
        out = jnp.einsum('bhnm,bhmd->bhnd', attn, v)
        out = out.transpose(0, 2, 1, 3).reshape(b, n, D_OUT)
        return out @ wo.T + bo
    x = _layernorm(x + _L0_gnn_ref(x, adj, L0_gnn_Wq, L0_gnn_bq, L0_gnn_Wk, L0_gnn_bk, L0_gnn_Wv, L0_gnn_bv, L0_gnn_Wo, L0_gnn_bo, L0_gnn_gamma, L0_gnn_beta), axis=-1)
    x = _layernorm(x + _L1_gnn_ref(x, adj, L1_gnn_wq, L1_gnn_bq, L1_gnn_wk, L1_gnn_bk, L1_gnn_wv, L1_gnn_bv, L1_gnn_wo, L1_gnn_bo), axis=-1)
    return x

_drawn_inputs = setup_inputs


def setup_inputs(seed=0):
    import zlib

    import numpy as np

    out = dict(_drawn_inputs(seed))
    spreads = {'L0_gnn_bq': (0.0, 0.8),
     'L0_gnn_bk': (0.0, 2.0),
     'L0_gnn_bv': (0.0, 0.1),
     'L0_gnn_bo': (0.0, 0.294),
     'L0_gnn_gamma': (1.0, 0.2),
     'L0_gnn_beta': (0.0, 0.1)}
    factors = {'L1_gnn_bq': 8.0, 'L1_gnn_bk': 64.0}
    for name, (base, spread) in spreads.items():
        noise = np.random.default_rng([zlib.crc32(name.encode()), seed]).standard_normal(out[name].shape)
        drawn = base * np.exp(spread * noise) if base else spread * noise
        out[name] = jnp.asarray(drawn.astype(out[name].dtype))
    for name, factor in factors.items():
        out[name] = (out[name] * factor).astype(out[name].dtype)
    return out
```

```python
from collections import namedtuple
from contextlib import ExitStack

import concourse.bass as bass
from concourse import mybir

F32 = mybir.dt.float32
F32R = mybir.dt.float32r
BF16 = mybir.dt.bfloat16
I8 = mybir.dt.int8
I32 = mybir.dt.int32
ALU = mybir.AluOpType
ACT = mybir.ActivationFunctionType
AX_X = mybir.AxisListType.X

P = 128
HEADS = 4
HD = P // HEADS
RING = 8
STAGE = 4
CLIP = 10.0
MASKED = -1e30
EPS = 1e-5
UNITS = 32
PAIRS = 16
SETUP_USES = 4
DMA = 16
STACK_DMAS = 16

Batch = namedtuple("Batch", "layer par g b turn first at")


def uses_of(batch, prev, nxt):
    order = []
    if prev is not None:
        order += (["R1"] if prev.layer else []) + ["Wo1"]
    if nxt is not None:
        order += ["X0", "X1", "Q0", "Q1", "K0", "K1"]
    if batch is not None and batch.layer:
        order += ["R0"]
    if nxt is not None:
        order += ["V0", "V1"]
    if batch is not None:
        order += ["Wo0"]
    return order


def wait(eng, sem, n):
    if isinstance(n, int) and n <= 0:
        return
    eng.wait_ge(sem, n)


def wait_alone(eng, sem, n, passed):
    wait(eng, sem, n)
    if not isinstance(n, int):
        eng.sem_inc(passed, 1)


def adj_block_kernel(
    nc, x, adj, wq0, bq0, wk0, bk0, wv0, bv0, wo0, bo0, gamma, beta,
    wq1, bq1, wk1, bk1, wv1, bv1, wo1, bo1, out, x1_dram,
):
    B, N, F = x.shape
    T = N // P
    assert F == P and T == 8 and B == 8
    SCALE = float(HD) ** -0.5
    HALF = N // 2

    x_view = x.rearrange("b (t p) f -> b p t f", p=P)
    x1_view = x1_dram.rearrange("b (t p) f -> b p t f", p=P)
    out_view = out.rearrange("b (t p) f -> b p t f", p=P)

    def one(view, b):
        return view[bass.ds(b, 1)].rearrange("o p t f -> (o p) t f")

    with ExitStack() as ctx:
        def sb(name, shape, dt=F32):
            return ctx.enter_context(nc.sbuf_tensor(name, shape, dt))

        def sem(name):
            return ctx.enter_context(nc.semaphore(name))

        clip_mask = sb("clip_mask", [P, T, N], I8)
        bias_mask = sb("bias_mask", [P, T, N], BF16)
        has_edge = sb("has_edge", [P, T])
        q_stack = [sb(f"q_stack{i}", [P, HEADS, N], F32R) for i in range(2)]
        k_stack = [sb(f"k_stack{i}", [P, HEADS, N], F32R) for i in range(2)]
        v_tok = [sb(f"v_tok{i}", [P, T, P]) for i in range(2)]
        stage = sb("stage", [P, STAGE, N])
        ring = sb("ring", [P, RING, N])
        x_in = sb("x_in", [P, T, P])
        x_t = sb("x_t", [P, N])
        hi = {"Q": sb("q_hi", [P, N], F32R), "K": sb("k_hi", [P, N], F32R)}
        lo = {"Q": sb("q_lo", [P, N], F32R), "K": sb("k_lo", [P, N], F32R)}
        x_res = sb("x_res", [P, T, P])
        x_bo = sb("x_bo", [P, T, P])
        y = [sb(f"y{i}", [P, T, P]) for i in range(2)]
        b_rows = y[1][0:1, :, :].rearrange("p t f -> p (t f)")
        norm_row = sb("norm_row", [P, 2, HALF])
        scaled = sb("scaled", [P, 2, HALF])
        ctx_t = sb("ctx_t", [P, 2, HALF])
        w_t = sb("w_t", [P, 2, 4, P])
        b_cols = sb("b_cols", [P, 4])
        b_all = sb("b_all", [P, 6, P])
        ident = sb("ident", [P, P])
        ident_bf = sb("ident_bf", [P, P], BF16)
        ones = sb("ones", [P, P])
        row_max = sb("row_max", [P, 2, UNITS])
        row_sum = sb("row_sum", [P, 2, UNITS])
        inv_sum = sb("inv_sum", [P, 16])
        stats = sb("stats", [P, T, 6])
        moments = sb("moments", [P, T, 2])
        rstd = sb("rstd", [P, T])
        power = sb("power", [P, T])

        score = ctx.enter_context(nc.psum_tensor("score", [P, 2, N], F32))
        acc = ctx.enter_context(nc.psum_tensor("acc", [P, 3, HALF], F32))
        work = ctx.enter_context(nc.psum_tensor("work", [P, HALF], F32))

        consts_made = sem("consts_made")
        weights_loaded = sem("weights_loaded")
        adj_loaded = sem("adj_loaded")
        setup_done = sem("setup_done")
        mask_biased = sem("mask_biased")
        mask_turned = sem("mask_turned")
        mask_clipped = sem("mask_clipped")
        xin_loaded = sem("xin_loaded")
        xres_loaded = sem("xres_loaded")
        q_stacked = sem("q_stacked")
        k_stacked = sem("k_stacked")
        stored = [sem(f"stored{i}") for i in range(2)]
        work_ready = sem("work_ready")
        work_read = sem("work_read")
        hi_ready = sem("hi_ready")
        xbo_ready = sem("xbo_ready")
        l0_scores = sem("l0_scores")
        l0_clipped = sem("l0_clipped")
        l0_exped = sem("l0_exped")
        l0_sums = sem("l0_sums")
        l0_ctx = sem("l0_ctx")
        l0_lned = sem("l0_lned")
        l0_inv = sem("l0_inv")
        l0_scaled = sem("l0_scaled")
        l0_summed = sem("l0_summed")
        l1_scores = sem("l1_scores")
        l1_masked = sem("l1_masked")
        l1_exped = sem("l1_exped")
        l1_turned = sem("l1_turned")
        l1_copied0 = sem("l1_copied0")
        l1_copied1 = sem("l1_copied1")
        l1_ctx = sem("l1_ctx")
        l1_recip = sem("l1_recip")
        l1_inv = sem("l1_inv")
        l1_expanded = sem("l1_expanded")
        l1_normed = sem("l1_normed")
        stats_made = sem("stats_made")
        moments_made = sem("moments_made")
        ln_steps = sem("ln_steps")

        waits_passed = {e: sem(f"waits_passed_{e}") for e in ("sp", "dve", "pool")}

        def ln_base(m):
            return 1 + (11 * m.b if m.layer == 0 else 11 * B + 4 * m.b)

        def moments_base(m):
            return 2 * m.b if m.layer == 0 else 2 * B + m.b

        def use(m, prev, nxt, name):
            return m.at + uses_of(m, prev, nxt).index(name) + 1

        def on_dve(u):
            return u % 4 != 3

        def walk(eng, body, prologue, epilogue):
            at0 = SETUP_USES + 8

            def batch(layer, par, b, turn):
                if layer == 0:
                    at = at0 if isinstance(b, int) and b == 0 else at0 - 1 + 10 * b
                else:
                    at = at0 - 1 + 10 * B if isinstance(b, int) and b == 0 else at0 - 2 + 10 * B + 12 * b
                return Batch(layer, par, b + B * layer, b, turn, isinstance(b, int) and b == 0, at)

            prologue(batch(0, 0, 0, 0))
            for layer in range(2):
                before = batch(0, 1, B - 1, B // 2 - 1) if layer else None
                body(batch(layer, 0, 0, 0), before, batch(layer, 1, 1, 0))
                with eng.Fori(0, (B - 2) // 2) as i:
                    odd, even = batch(layer, 1, 2 * i + 1, i), batch(layer, 0, 2 * i + 2, i + 1)
                    body(odd, batch(layer, 0, 2 * i, i), even)
                    body(even, odd, batch(layer, 1, 2 * i + 3, i + 1))
                last = batch(layer, 1, B - 1, B // 2 - 1)
                body(last, batch(layer, 0, B - 2, B // 2 - 1), batch(1, 0, 0, 0) if layer == 0 else None)
            epilogue(last)

        def last_at():
            return SETUP_USES + 8 - 2 + 10 * B + 12 * (B - 1) + 4

        TAIL = range(UNITS, UNITS + 7)

        def at_once(m):
            return m.layer == 1 and m.first

        block = ctx.enter_context(nc.Block())

        @block.sync
        def _(sp):
            for half in stored:
                sp.sem_inc(half, DMA)
            w_in = x_t[:, :].rearrange("p (l m f) -> p l m f", l=2, m=4)
            for i, w in enumerate((wq0, wk0, wv0, wo0, wq1, wk1, wv1, wo1)):
                sp.dma_start(w_in[:, i // 4, i % 4, :], w).then_inc(weights_loaded, DMA)
            for i, v in enumerate((bq0, bk0, bq1, bk1)):
                sp.dma_start(b_cols[:, i:i + 1], v.rearrange("(d a) -> d a", a=1)).then_inc(weights_loaded, DMA)
            for i, v in enumerate((bo0, bo1, bv0, bv1, gamma, beta)):
                sp.dma_start(b_rows[0:1, i * P:(i + 1) * P], v.rearrange("(a d) -> a d", a=1)).then_inc(weights_loaded, DMA)
            adj_view = adj.rearrange("(t p) k -> p t k", p=P)
            adj_in = ring[:, :, :].bitcast(I32)
            sp.dma_start(x_in[:, :, :], x_view[0]).then_inc(xin_loaded, DMA)
            for t in range(T):
                sp.dma_start(adj_in[:, t, :], adj_view[:, t, :]).then_inc(adj_loaded, DMA)

            def stack(m, which, base, first_use):
                dst = (q_stack if which == "Q" else k_stack)[m.par]
                done = q_stacked if which == "Q" else k_stacked
                slots = (hi, hi, lo, lo) if which == "Q" else (hi, lo, hi, lo)
                wait_alone(sp, work_read, first_use + 1, waits_passed["sp"])
                if m.layer == 0:
                    wait_alone(sp, l0_scores, UNITS * (m.b - 1), waits_passed["sp"])
                else:
                    wait_alone(sp, l0_scores, UNITS * B - UNITS * (1 if m.first else 0), waits_passed["sp"])
                    wait_alone(sp, l1_scores, UNITS * (m.b - 1), waits_passed["sp"])
                for j, part in enumerate(slots):
                    for h in range(HEADS):
                        sp.dma_start(dst[HD * j:HD * j + HD, h, :].bitcast(F32),
                                     part[which][HD * h:HD * h + HD, :].bitcast(F32)).then_inc(done, DMA)

            def load_residual(m, prev):
                if m.layer == 1:
                    wait_alone(sp, stored[m.par], DMA * (m.turn + 2), waits_passed["sp"])
                source = x_view if m.layer == 0 else x1_view
                if prev is not None:
                    wait_alone(sp, xbo_ready, m.g, waits_passed["sp"])
                    if prev.layer == 0:
                        wait_alone(sp, ln_steps, ln_base(prev) + 7, waits_passed["sp"])
                sp.dma_start(x_res[:, :, :], one(source, m.b) if not m.first else source[0]).then_inc(xres_loaded, DMA)

            def store(m):
                target = x1_view if m.layer == 0 else out_view
                wait_alone(sp, ln_steps, ln_base(m) + (11 if m.layer == 0 else 4), waits_passed["sp"])
                sp.dma_start(one(target, m.b), y[m.par][:, :, :]).then_inc(stored[m.par], DMA)

            def body(m, prev, nxt):
                if nxt is not None:
                    wait_alone(sp, hi_ready, 4 * m.g + 4, waits_passed["sp"])
                    if nxt.layer == 1:
                        wait_alone(sp, stored[nxt.par], DMA * (nxt.turn + 2), waits_passed["sp"])
                    source = x_view if nxt.layer == 0 else x1_view
                    sp.dma_start(x_in[:, :, :], one(source, nxt.b)).then_inc(xin_loaded, DMA)
                    stack(nxt, "Q", m, use(m, prev, nxt, "Q0"))
                    stack(nxt, "K", m, use(m, prev, nxt, "K0"))
                load_residual(m, prev)
                if prev is not None:
                    store(prev)

            def prologue(m):
                stack(m, "Q", m, SETUP_USES + 3)
                stack(m, "K", m, SETUP_USES + 5)

            def epilogue(m):
                store(m)
                for half in stored:
                    sp.wait_ge(half, DMA * (B + 1))

            walk(sp, body, prologue, epilogue)

        @block.tensor
        def _(pe):
            def fill(n, at=None):
                wait(pe, work_read, n - 1)

            def turn_tile(out, tile):
                return pe.transpose(out, tile, ident[:, :])

            pe.wait_ge(consts_made, 5)
            pe.wait_ge(weights_loaded, DMA * 18)
            for layer in range(2):
                fill(layer + 1)
                for m in range(4):
                    mm = turn_tile(work[:, m * P:(m + 1) * P],
                                   x_t[:, (layer * 4 + m) * P:(layer * 4 + m + 1) * P])
                mm.then_inc(work_ready, 1)
            for i, (a, b) in enumerate(((0, 4), (4, 6))):
                fill(3 + i)
                pe.matmul(work[:, 0:(b - a) * P], ones[0:1, :], b_rows[0:1, a * P:b * P],
                          start=True, stop=True).then_inc(work_ready, 1)

            def prep(m, name, n):
                half = int(name[1])
                cols = slice(half * HALF, (half + 1) * HALF)
                fill(n)
                if name[0] == "X":
                    if half == 0:
                        pe.wait_ge(xin_loaded, DMA * (m.g + 1))
                    for t in range(4):
                        mm = turn_tile(work[:, t * P:(t + 1) * P], x_in[:, 4 * half + t, :])
                elif name[0] == "V":
                    for t in range(4):
                        mm = pe.matmul(work[:, t * P:(t + 1) * P], x_t[:, (4 * half + t) * P:(4 * half + t + 1) * P],
                                       w_t[:, m.layer, 2, :], start=True, stop=True)
                else:
                    mm = pe.matmul(work[:, :], w_t[:, m.layer, "QK".index(name[0]), :], x_t[:, cols],
                                   start=True, stop=True)
                mm.then_inc(work_ready, 1)

            def project(m, half, n):
                fill(n)
                if m.layer == 0:
                    pe.wait_ge(l0_summed, 14 * m.b + 7 * (half + 1))
                else:
                    pe.wait_ge(l1_normed, 2 * m.b + half + 1)
                for t in range(4):
                    mm = pe.matmul(work[:, t * P:(t + 1) * P], ctx_t[:, half, t * P:(t + 1) * P],
                                   w_t[:, m.layer, 3, :], start=True, stop=True)
                mm.then_inc(work_ready, 1)

            def turn_inverse(m, half, n):
                fill(n)
                pe.wait_ge(l1_expanded, 2 * m.b + half + 1)
                for t in range(4):
                    mm = turn_tile(work[:, t * P:(t + 1) * P], norm_row[:, 0, t * P:(t + 1) * P])
                mm.then_inc(work_ready, 1)

            def scores(m, u):
                if u == 0:
                    pe.wait_ge(q_stacked, DMA * STACK_DMAS * (m.g + 1))
                    pe.wait_ge(k_stacked, DMA * STACK_DMAS * (m.g + 1))
                    if m.layer == 0 and m.first:
                        pe.wait_ge(mask_clipped, T)
                    if m.layer == 1 and m.first:
                        pe.wait_ge(l0_clipped, UNITS * B)
                qs, ks = q_stack[m.par], k_stack[m.par]
                if m.layer == 0:
                    wait(pe, l0_clipped, UNITS * m.b + u - 1)
                    half, kt, hp = u // 16, u // 2 % 8, u % 2
                    for i in range(2):
                        h = 2 * hp + i
                        mm = pe.matmul(score[:, u % 2, i * HALF:(i + 1) * HALF], ks[:, h, kt * P:(kt + 1) * P],
                                       qs[:, h, half * HALF:(half + 1) * HALF], start=True, stop=True)
                    mm.then_inc(l0_scores, 1)
                else:
                    wait(pe, l1_masked, UNITS * m.b + u - 1)
                    qt, h = u // 4, u % 4
                    for i in range(2):
                        mm = pe.matmul(score[:, u % 2, i * HALF:(i + 1) * HALF], qs[:, h, qt * P:(qt + 1) * P],
                                       ks[:, h, i * HALF:(i + 1) * HALF], start=True, stop=True)
                    mm.then_inc(l1_scores, 1)

            def pair(m, p):
                pe.wait_ge(l0_exped, UNITS * m.b + 2 * p + 2)
                for what in range(2):
                    if (what == 0) == (p == 0):
                        wait(pe, l0_lned, PAIRS * m.b + p)
                    else:
                        wait(pe, l0_scaled, PAIRS * m.b + (p - 1 if p else 0))
                    bank = (2 * p + what) % 3
                    for h in range(HEADS):
                        u = 2 * p + h // 2
                        w = v_tok[m.par][:, p % 8, HD * h:HD * h + HD] if what else ones[:, 0:HD]
                        mm = pe.matmul(acc[HD * h:HD * h + HD, bank, :], w,
                                       ring[:, u % RING, (h % 2) * HALF:(h % 2 + 1) * HALF],
                                       start=True, stop=True)
                    mm.then_inc(l0_ctx if what else l0_sums, 1)

            def turn(m, u):
                pe.wait_ge(l1_exped, UNITS * m.b + u + 1)
                if m.first and u == 0:
                    pe.wait_ge(l0_lned, PAIRS * B)
                    pe.wait_ge(l0_scaled, PAIRS * B)
                for c in range(2):
                    wait(pe, (l1_copied0, l1_copied1)[c], UNITS * m.b + u)
                    for t in range(4):
                        mm = turn_tile(acc[:, c, t * P:(t + 1) * P],
                                       stage[:, u % STAGE, (4 * c + t) * P:(4 * c + t + 1) * P])
                    mm.then_inc(l1_turned, 1)

            def context(m, qt, part):
                if part == 0:
                    pe.wait_ge(l1_copied0, UNITS * m.b + 4 * qt + 4)
                    pe.wait_ge(l1_copied1, UNITS * m.b + 4 * qt + 4)
                    if qt % 4 == 0:
                        wait(pe, l1_normed, 2 * m.b + qt // 4)
                for kt in ((0, 1, 2), (3, 4, 5), (6, 7))[part]:
                    for h in range(HEADS):
                        mm = pe.matmul(acc[HD * h:HD * h + HD, 2, (qt % 4) * P:(qt % 4 + 1) * P],
                                       v_tok[m.par][:, kt, HD * h:HD * h + HD],
                                       ring[:, (4 * qt + h) % RING, kt * P:(kt + 1) * P],
                                       start=(kt == 0), stop=(kt == T - 1))
                if part == 2:
                    mm.then_inc(l1_ctx, 1)

            def attend(m, s):
                if m.layer == 0:
                    if s % 2 and 5 <= s <= 35:
                        pair(m, (s - 5) // 2)
                else:
                    if 3 <= s < UNITS + 3:
                        turn(m, s - 3)
                    if 7 <= s < UNITS + 6 and (s - 7) % 4 < 3:
                        context(m, (s - 7) // 4, (s - 7) % 4)

            PREP_AT = {10: "X0", 11: "X1", 12: "Q0", 14: "Q1", 16: "K0", 18: "K1", 22: "V0", 24: "V1"}

            def body(m, prev, nxt):
                if at_once(m):
                    for s in TAIL:
                        attend(prev, s)
                for s in range(UNITS):
                    scores(m, s)
                    if prev is not None:
                        if not at_once(m):
                            attend(prev, s + UNITS)
                        if prev.layer and s == 5:
                            turn_inverse(prev, 1, use(m, prev, nxt, "R1"))
                        if s == 8:
                            project(prev, 1, use(m, prev, nxt, "Wo1"))
                    attend(m, s)
                    if nxt is not None and s in PREP_AT:
                        prep(nxt, PREP_AT[s], use(m, prev, nxt, PREP_AT[s]))
                    if m.layer and s == 20:
                        turn_inverse(m, 0, use(m, prev, nxt, "R0"))
                    if s == 27:
                        project(m, 0, use(m, prev, nxt, "Wo0"))

            def prologue(m):
                for i, name in enumerate(("X0", "X1", "Q0", "Q1", "K0", "K1", "V0", "V1")):
                    prep(m, name, SETUP_USES + 1 + i)
                score_bf = score[:, :, :].bitcast(BF16).rearrange("p a (c n) -> p (a c) n", c=2)
                pe.wait_ge(mask_biased, T)
                for kt in range(T):
                    wait(pe, mask_clipped, kt - 3)
                    for qt in range(T):
                        mm = pe.transpose(score_bf[:, kt % 4, qt * P:(qt + 1) * P],
                                          bias_mask[:, qt, kt * P:(kt + 1) * P], ident_bf[:, :])
                    mm.then_inc(mask_turned, 1)

            def epilogue(m):
                for s in range(UNITS, UNITS + 6):
                    attend(m, s)
                turn_inverse(m, 1, last_at() + 1)
                project(m, 1, last_at() + 2)

            walk(pe, body, prologue, epilogue)

        @block.vector
        def _(dve):
            for layer in range(2):
                dve.wait_ge(work_ready, layer + 1)
                dve.tensor_scalar(w_t[:, layer, 0, :], work[:, 0:P], SCALE, None, ALU.mult)
                dve.tensor_copy(w_t[:, layer, 1:4, :],
                                work[:, P:4 * P].rearrange("p (m f) -> p m f", m=3)).then_inc(work_read, 1)
            for i, (a, b) in enumerate(((0, 4), (4, 6))):
                dve.wait_ge(work_ready, 3 + i)
                dve.tensor_copy(b_all[:, a:b, :], work[:, 0:(b - a) * P].rearrange("p (m f) -> p m f", f=P))\
                   .then_inc(work_read, 1)
            dve.tensor_scalar(b_cols[:, 0:4:2], b_cols[:, 0:4:2], SCALE, None, ALU.mult).then_inc(setup_done, 1)
            adj_in = ring[:, :, :].bitcast(I32)
            score_bf = score[:, :, :].bitcast(BF16).rearrange("p a (c n) -> p (a c) n", c=2)

            def clip_masks():
                for t in range(T):
                    if t == 0:
                        dve.wait_ge(adj_loaded, DMA * T)
                    dve.tensor_scalar(bias_mask[:, t, :], adj_in[:, t, :], 0.0, MASKED, ALU.is_equal, ALU.mult)\
                       .then_inc(mask_biased, 1)
                dve.wait_ge(mask_biased, T)
                dve.tensor_reduce(has_edge[:, :], bias_mask[:, :, :], AX_X, ALU.max).then_inc(setup_done, 1)
                dve.wait_ge(setup_done, 2)
                dve.tensor_scalar(has_edge[:, :], has_edge[:, :], 0.0, None, ALU.is_equal).then_inc(setup_done, 1)
                for kt in range(T):
                    dve.wait_ge(mask_turned, kt + 1)
                    dve.tensor_scalar(clip_mask[:, kt, :], score_bf[:, kt % 4, :], -2 * CLIP, CLIP,
                                      ALU.max, ALU.add).then_inc(mask_clipped, 1)

            def low_part(m, name, n):
                which, half = name[0], int(name[1])
                cols = slice(half * HALF, (half + 1) * HALF)
                k = ("Q0", "Q1", "K0", "K1").index(name)
                dve.wait_ge(hi_ready, 4 * m.g + k + 1)
                c = 2 * m.layer + "QK".index(which)
                dve.scalar_tensor_tensor(out=lo[which][:, cols], in0=work[:, :], scalar=b_cols[:, c:c + 1],
                                         in1=hi[which][:, cols].bitcast(F32), op0=ALU.add, op1=ALU.subtract)\
                   .then_inc(work_read, 1)

            def take_v(m, half, n):
                dve.wait_ge(work_ready, n)
                if m.layer == 0:
                    wait(dve, l0_ctx, PAIRS * (m.b - 1))
                else:
                    dve.wait_ge(l0_ctx, PAIRS * B - PAIRS * (1 if m.first else 0))
                    wait(dve, l1_ctx, T * (m.b - 1))
                dve.tensor_tensor(v_tok[m.par][:, 4 * half:4 * half + 4, :],
                                  work[:, :].rearrange("p (t f) -> p t f", t=4),
                                  b_all[:, 2 + m.layer, :][:, None, :].to_broadcast([P, 4, P]), ALU.add)\
                   .then_inc(work_read, 1)

            def clip(m, u):
                dve.wait_ge(l0_scores, UNITS * m.b + u + 1)
                wait(dve, l0_exped, UNITS * m.b + u - STAGE + 1)
                half, kt = u // 16, u // 2 % 8
                dve.scalar_tensor_tensor(
                    out=stage[:, u % STAGE, :].rearrange("p (h n) -> p h n", h=2),
                    in0=score[:, u % 2, :].rearrange("p (h n) -> p h n", h=2), scalar=-CLIP,
                    in1=clip_mask[:, kt, half * HALF:(half + 1) * HALF][:, None, :].to_broadcast([P, 2, HALF]),
                    op0=ALU.max, op1=ALU.min).then_inc(l0_clipped, 1)

            def scale_pair(m, p):
                dve.wait_ge(l0_ctx, PAIRS * m.b + p + 1)
                dve.wait_ge(l0_inv, PAIRS * m.b + p + 1)
                half, kt = p // 8, p % 8
                if kt == 0:
                    target = ctx_t[:, half, :]
                else:
                    target = scaled[:, p % 2, :]
                    adds = 7 * half + kt - 1
                    wait(dve, l0_summed, 14 * m.b + adds - (1 if kt > 1 else 0))
                dve.tensor_tensor(target, acc[:, (2 * p + 1) % 3, :], norm_row[:, p % 2, :], ALU.mult)\
                   .then_inc(l0_scaled, 1)

            def mask_max(m, u):
                dve.wait_ge(l1_scores, UNITS * m.b + u + 1)
                wait_alone(dve, l1_turned, 2 * (UNITS * m.b + u - STAGE + 1), waits_passed["dve"])
                if m.first and u == 0:
                    dve.wait_ge(l0_exped, UNITS * B)
                dve.tensor_tensor_reduce(
                    out=stage[:, u % STAGE, :], in0=score[:, u % 2, :], in1=bias_mask[:, u // 4, :],
                    scale=-1.0, scalar=3e38, op0=ALU.add, op1=ALU.min,
                    accum_out=row_max[:, m.par, u:u + 1]).then_inc(l1_masked, 1)

            def copy_turned(m, u):
                dve.wait_ge(l1_turned, 2 * (UNITS * m.b + u + 1))
                wait(dve, l1_ctx, T * m.b + u // 4 - 1)
                dve.tensor_copy(ring[:, u % RING, HALF:N], acc[:, 1, :]).then_inc(l1_copied1, 1)

            def invert(m, half):
                dve.wait_ge(l1_exped, UNITS * m.b + 16 * (half + 1))
                wait(dve, l1_expanded, 2 * m.b + half)
                dve.reciprocal(inv_sum[:, :], row_sum[:, m.par, 16 * half:16 * half + 16]).then_inc(l1_recip, 1)

            def normalise(m, half, n):
                dve.wait_ge(l1_ctx, T * m.b + 4 * (half + 1))
                dve.wait_ge(work_read, n)
                dve.tensor_tensor(ctx_t[:, half, :], acc[:, 2, :], norm_row[:, 1, :], ALU.mult).then_inc(l1_normed, 1)

            def add_residual(m, half, n):
                dve.wait_ge(work_ready, n)
                if half == 0:
                    dve.wait_ge(xbo_ready, m.g + 1)
                    wait(dve, stored[m.par], DMA * (m.turn + B // 2 * m.layer + 1))
                dve.tensor_tensor(y[m.par][:, 4 * half:4 * half + 4, :],
                                  work[:, :].rearrange("p (t f) -> p t f", t=4),
                                  x_bo[:, 4 * half:4 * half + 4, :], ALU.add).then_inc(work_read, 1)

            def layer_stats(m, which, n):
                if which == 0:
                    dve.wait_ge(work_read, n)
                    wait(dve, ln_steps, ln_base(m))
                else:
                    dve.wait_ge(ln_steps, ln_base(m) + 7)
                base = moments_base(m) + which
                for t in range(T):
                    dve.bn_stats(stats[:, t, :], y[m.par][:, t, :]).then_inc(stats_made, 1)
                wait_alone(dve, stats_made, T * (base + 1), waits_passed["dve"])
                for t in range(T):
                    mm = dve.bn_aggr(moments[:, t, :], stats[:, t, :])
                mm.then_inc(moments_made, 1)

            def attend(m, s, n_r=(None, None)):
                if m.layer == 0:
                    if s % 2 == 0 and 6 <= s <= 36:
                        scale_pair(m, (s - 6) // 2)
                else:
                    if 2 <= s < UNITS + 2 and on_dve(s - 2):
                        copy_turned(m, s - 2)

            LOW_AT = {12: "Q0", 14: "Q1", 16: "K0", 18: "K1"}
            V_AT = {22: 0, 24: 1}

            def body(m, prev, nxt):
                if at_once(m):
                    for s in TAIL:
                        attend(prev, s)
                for s in range(UNITS):
                    (mask_max if m.layer else clip)(m, s)
                    if prev is not None:
                        if not at_once(m):
                            attend(prev, s + UNITS)
                        if prev.layer and s == 1:
                            invert(prev, 1)
                        if prev.layer and s == 5:
                            normalise(prev, 1, use(m, prev, nxt, "R1"))
                        if s == 8:
                            add_residual(prev, 1, use(m, prev, nxt, "Wo1"))
                        if s == 9:
                            layer_stats(prev, 0, use(m, prev, nxt, "Wo1"))
                        if prev.layer == 0 and s == 22:
                            layer_stats(prev, 1, None)
                    if nxt is not None:
                        if s in LOW_AT:
                            low_part(nxt, LOW_AT[s], use(m, prev, nxt, LOW_AT[s]))
                        if s in V_AT:
                            take_v(nxt, V_AT[s], use(m, prev, nxt, f"V{V_AT[s]}"))
                    if m.layer and s == 17:
                        invert(m, 0)
                    if m.layer and s == 21:
                        normalise(m, 0, use(m, prev, nxt, "R0"))
                    if s == 27:
                        add_residual(m, 0, use(m, prev, nxt, "Wo0"))
                    attend(m, s)

            def prologue(m):
                for i, name in enumerate(("Q0", "Q1", "K0", "K1")):
                    low_part(m, name, SETUP_USES + 3 + i)
                for half in range(2):
                    take_v(m, half, SETUP_USES + 7 + half)
                clip_masks()

            def epilogue(m):
                for s in range(UNITS, UNITS + 2):
                    attend(m, s)
                invert(m, 1)
                normalise(m, 1, last_at() + 1)
                add_residual(m, 1, last_at() + 2)
                layer_stats(m, 0, last_at() + 2)

            walk(dve, body, prologue, epilogue)

        @block.scalar
        def _(act):
            act.preload_act_table_set("natural_log_exp_and_others")

            def take_x(half, n):
                act.wait_ge(work_ready, n)
                act.activation(x_t[:, half * HALF:(half + 1) * HALF], work[:, :], ACT.Copy).then_inc(work_read, 1)

            def high_part(m, name, n):
                which, half = name[0], int(name[1])
                act.wait_ge(work_ready, n)
                wait(act, q_stacked if which == "Q" else k_stacked, DMA * STACK_DMAS * m.g)
                c = 2 * m.layer + "QK".index(which)
                act.activation(hi[which][:, half * HALF:(half + 1) * HALF], work[:, :], ACT.Identity,
                               bias=b_cols[:, c:c + 1]).then_inc(hi_ready, 1)

            def exp0(m, u):
                act.wait_ge(l0_clipped, UNITS * m.b + u + 1)
                wait(act, l0_ctx, PAIRS * m.b + u // 2 - 3)
                act.activation(ring[:, u % RING, :], stage[:, u % STAGE, :], ACT.Exp).then_inc(l0_exped, 1)

            def log_sums(m, p):
                act.wait_ge(l0_sums, PAIRS * m.b + p + 1)
                wait(act, l0_scaled, PAIRS * m.b + p - 1)
                act.activation(norm_row[:, p % 2, :], acc[:, (2 * p) % 3, :], ACT.Ln).then_inc(l0_lned, 1)

            def inverse_sums(m, p):
                act.wait_ge(l0_lned, PAIRS * m.b + p + 1)
                act.activation(norm_row[:, p % 2, :], norm_row[:, p % 2, :], ACT.Exp, scale=-1.0).then_inc(l0_inv, 1)

            def exp1(m, u):
                act.wait_ge(l1_masked, UNITS * m.b + u + 1)
                act.activation(stage[:, u % STAGE, :], stage[:, u % STAGE, :], ACT.Exp,
                               bias=row_max[:, m.par, u:u + 1], scale=-1.0,
                               accum_out=row_sum[:, m.par, u:u + 1]).then_inc(l1_exped, 1)

            def copy_turned(m, u, c):
                act.wait_ge(l1_turned, 2 * (UNITS * m.b + u) + c + 1)
                wait(act, l1_ctx, T * m.b + u // 4 - 1)
                act.activation(ring[:, u % RING, c * HALF:(c + 1) * HALF], acc[:, c, :], ACT.Copy)\
                   .then_inc((l1_copied0, l1_copied1)[c], 1)

            def take_inverse(m, half, n):
                act.wait_ge(work_ready, n)
                wait(act, l1_normed, 2 * m.b + half)
                act.activation(norm_row[:, 1, :], work[:, :], ACT.Copy).then_inc(work_read, 1)

            def attend(m, s):
                if m.layer == 1 and 1 <= s < UNITS + 1:
                    copy_turned(m, s - 1, 0)
                    if not on_dve(s - 1):
                        copy_turned(m, s - 1, 1)

            def pair_before(m, s):
                if m is not None and m.layer == 0 and s % 2 == 0 and 4 <= s <= 34:
                    log_sums(m, (s - 4) // 2)

            def pair_after(m, s):
                if m is not None and m.layer == 0 and s % 2 == 0 and 4 <= s <= 34:
                    inverse_sums(m, (s - 4) // 2)

            def body(m, prev, nxt):
                if at_once(m):
                    for s in TAIL:
                        pair_before(prev, s)
                        pair_after(prev, s)
                for s in range(UNITS):
                    if not at_once(m):
                        pair_before(prev, s + UNITS)
                    pair_before(m, s)
                    if prev is not None and prev.layer and s == 4:
                        take_inverse(prev, 1, use(m, prev, nxt, "R1"))
                    if nxt is not None:
                        if s in (9, 10):
                            take_x(s - 9, use(m, prev, nxt, f"X{s - 9}"))
                        if s in (11, 13, 15, 17):
                            name = {11: "Q0", 13: "Q1", 15: "K0", 17: "K1"}[s]
                            high_part(nxt, name, use(m, prev, nxt, name))
                    if m.layer and s == 19:
                        take_inverse(m, 0, use(m, prev, nxt, "R0"))
                    (exp1 if m.layer else exp0)(m, s)
                    if not at_once(m):
                        pair_after(prev, s + UNITS)
                    pair_after(m, s)
                    if prev is not None:
                        attend(prev, s + UNITS)
                    attend(m, s)

            def prologue(m):
                act.wait_ge(setup_done, 1)
                for half in range(2):
                    take_x(half, SETUP_USES + 1 + half)
                for i, name in enumerate(("Q0", "Q1", "K0", "K1")):
                    high_part(m, name, SETUP_USES + 3 + i)
                act.wait_ge(mask_biased, T)

            def epilogue(m):
                attend(m, UNITS)
                take_inverse(m, 1, last_at() + 1)

            walk(act, body, prologue, epilogue)

        @block.gpsimd
        def _(pool):
            pool.memset(ident[:, :], 0.0).then_inc(consts_made, 1)
            pool.memset(ones[:, :], 1.0).then_inc(consts_made, 1)
            pool.memset(power[:, :], -0.5).then_inc(consts_made, 1)
            pool.wait_ge(consts_made, 3)
            pool.affine_select(out=ident[:, :], in_=ident[:, :], compare_op=ALU.not_equal, fill=1.0, base=0,
                               pattern=[[-1, P]], channel_multiplier=1).then_inc(consts_made, 1)
            pool.wait_ge(consts_made, 4)
            pool.tensor_copy(ident_bf[:, :], ident[:, :]).then_inc(consts_made, 1)
            pool.sem_inc(ln_steps, 1)

            def spread(row):
                return row[:, None, :].to_broadcast([P, T, P])

            def per_token(col):
                return col[:, :, None].to_broadcast([P, T, P])

            def add_bias(m, prev, n_free):
                pool.wait_ge(xres_loaded, DMA * (m.g + 1))
                if prev is not None:
                    pool.wait_ge(work_read, n_free)
                else:
                    pool.wait_ge(work_read, 3)
                pool.tensor_tensor(x_bo[:, :, :], x_res[:, :, :], spread(b_all[:, m.layer, :]), ALU.add)\
                    .then_inc(xbo_ready, 1)

            def step(op, m, k):
                if k > 1:
                    wait_alone(pool, ln_steps, ln_base(m) + k - 1, waits_passed["pool"])
                op().then_inc(ln_steps, 1)

            def norm(m, k0, which):
                wait_alone(pool, moments_made, moments_base(m) + which + 1, waits_passed["pool"])
                yt = y[m.par][:, :, :]
                step(lambda: pool.tensor_scalar(rstd[:, :], moments[:, :, 1], EPS, 1.0, ALU.add, ALU.mult), m, k0)
                step(lambda: pool.tensor_tensor(rstd[:, :], rstd[:, :], power[:, :], ALU.pow), m, k0 + 1)
                step(lambda: pool.tensor_tensor(yt, yt, per_token(moments[:, :, 0]), ALU.subtract), m, k0 + 2)
                step(lambda: pool.tensor_tensor(yt, yt, per_token(rstd[:, :]), ALU.mult), m, k0 + 3)

            def affine_residual(m):
                yt = y[m.par][:, :, :]
                step(lambda: pool.tensor_tensor(yt, yt, spread(b_all[:, 4, :]), ALU.mult), m, 5)
                step(lambda: pool.tensor_tensor(yt, yt, spread(b_all[:, 5, :]), ALU.add), m, 6)
                step(lambda: pool.tensor_tensor(yt, yt, x_res[:, :, :], ALU.add), m, 7)

            def sum_pair(m, p):
                half, kt = p // 8, p % 8
                pool.wait_ge(l0_scaled, PAIRS * m.b + p + 1)
                if kt:
                    wait(pool, l0_summed, 14 * m.b + 7 * half + kt - 1)
                    pool.tensor_tensor(ctx_t[:, half, :], ctx_t[:, half, :], scaled[:, p % 2, :], ALU.add)\
                        .then_inc(l0_summed, 1)

            def expand(m, half, n_free):
                pool.wait_ge(l1_recip, 2 * m.b + half + 1)
                if m.first and half == 0:
                    pool.wait_ge(l0_scaled, PAIRS * B)
                elif n_free is not None:
                    pool.wait_ge(work_ready, n_free)
                for t in range(4):
                    mm = pool.tensor_tensor(
                        norm_row[:, 0, t * P:(t + 1) * P].rearrange("p (h d) -> p h d", h=HEADS),
                        inv_sum[:, 4 * t:4 * t + 4][:, :, None].to_broadcast([P, HEADS, HD]),
                        has_edge[:, 4 * half + t:4 * half + t + 1][:, :, None].to_broadcast([P, HEADS, HD]),
                        ALU.mult)
                mm.then_inc(l1_expanded, 1)

            def attend(m, s):
                if m.layer == 0 and s % 2 == 0 and 8 <= s <= 38:
                    sum_pair(m, (s - 8) // 2)

            def body(m, prev, nxt):
                if at_once(m):
                    for s in TAIL:
                        attend(prev, s)
                for s in range(UNITS):
                    if prev is not None:
                        if not at_once(m):
                            attend(prev, s + UNITS)
                        if prev.layer and s == 2:
                            expand(prev, 1, prev.at + uses_of(prev, prev, m).index("R0") + 1 - (1 if prev.first else 0))
                    attend(m, s)
                    if prev is not None:
                        if s == 11:
                            norm(prev, 1, 0)
                        if s == 15 and prev.layer == 0:
                            affine_residual(prev)
                        if s == 23 and prev.layer == 0:
                            norm(prev, 8, 1)
                    if m.layer and s == 18:
                        expand(m, 0, use(m, prev, nxt, "R1") if prev.layer else None)
                    if s == 20:
                        add_bias(m, prev, use(m, prev, nxt, "Wo1") if prev is not None else None)

            def prologue(m):
                pass

            def epilogue(m):
                expand(m, 1, m.at + 3)
                norm(m, 1, 0)

            walk(pool, body, prologue, epilogue)


_INS = ["x", "adj"] + [f"L0_gnn_{n}" for n in ("Wq", "bq", "Wk", "bk", "Wv", "bv", "Wo", "bo", "gamma", "beta")] \
    + [f"L1_gnn_{n}" for n in ("wq", "bq", "wk", "bk", "wv", "bv", "wo", "bo")]


def kernel(**inputs):
    import numpy as _np
    import concourse.bacc as _bacc
    from concourse import mybir as _mybir
    from concourse.bass_utils import run_bass_kernel_spmd as _run

    nc = _bacc.Bacc("TRN2", target_bir_lowering=False, num_devices=1)
    arrays, args = {}, []
    for name in _INS:
        a = _np.ascontiguousarray(inputs[name])
        arrays[f"in_{name}"] = a
        args.append(nc.dram_tensor(f"in_{name}", a.shape, _mybir.dt.from_np(a.dtype), kind="ExternalInput").ap())
    shape = tuple(inputs["x"].shape)
    out = nc.dram_tensor("out_0", shape, _mybir.dt.float32, kind="ExternalOutput").ap()
    x1 = nc.dram_tensor("x1_scratch", shape, _mybir.dt.float32, kind="Internal").ap()
    adj_block_kernel(nc, *args, out, x1)
    r = _run(nc, [arrays], core_ids=[0])
    return r.results[0]["out_0"]
```

```python
from collections import namedtuple
from contextlib import ExitStack

import concourse.bass as bass
from concourse import mybir

F32 = mybir.dt.float32
F32R = mybir.dt.float32r
BF16 = mybir.dt.bfloat16
I8 = mybir.dt.int8
I32 = mybir.dt.int32
ALU = mybir.AluOpType
ACT = mybir.ActivationFunctionType
AX_X = mybir.AxisListType.X

P = 128
HEADS = 4
HD = P // HEADS
RING = 8
STAGE = 4
CLIP = 10.0
MASKED = -1e30
EPS = 1e-5
UNITS = 32
PAIRS = 16
DMA = 16
STACK_DMAS = 16

Batch = namedtuple("Batch", "layer par g b turn first at")


def uses_of(batch, prev, nxt):
    order = []
    if prev is not None:
        order += (["R1"] if prev.layer else []) + ["Wo1"]
    if nxt is not None:
        order += ["X0", "X1", "Q0", "Q1", "K0", "K1"]
    if batch is not None and batch.layer:
        order += ["R0"]
    if nxt is not None:
        order += ["V0", "V1"]
    if batch is not None:
        order += ["Wo0"]
    return order


def wait(eng, sem, n):
    if isinstance(n, int) and n <= 0:
        return
    eng.wait_ge(sem, n)


def wait_alone(eng, sem, n, passed):
    wait(eng, sem, n)
    if not isinstance(n, int):
        eng.sem_inc(passed, 1)


def adj_block_kernel(
    nc, x, adj, wq0, bq0, wk0, bk0, wv0, bv0, wo0, bo0, gamma, beta,
    wq1, bq1, wk1, bk1, wv1, bv1, wo1, bo1, out, x1_dram,
):
    B, N, F = x.shape
    T = N // P
    assert F == P and T == 8 and B == 8
    SCALE = float(HD) ** -0.5
    HALF = N // 2

    x_view = x.rearrange("b (t p) f -> b p t f", p=P)
    x1_view = x1_dram.rearrange("b (t p) f -> b p t f", p=P)
    out_view = out.rearrange("b (t p) f -> b p t f", p=P)

    def one(view, b):
        return view[bass.ds(b, 1)].rearrange("o p t f -> (o p) t f")

    with ExitStack() as ctx:
        def sb(name, shape, dt=F32):
            return ctx.enter_context(nc.sbuf_tensor(name, shape, dt))

        def sem(name):
            return ctx.enter_context(nc.semaphore(name))

        clip_mask = sb("clip_mask", [P, T, N], I8)
        bias_mask = sb("bias_mask", [P, T, N], BF16)
        q_stack = [sb(f"q_stack{i}", [P, HEADS, N], F32R) for i in range(2)]
        k_stack = [sb(f"k_stack{i}", [P, HEADS, N], F32R) for i in range(2)]
        v_tok = [sb(f"v_tok{i}", [P, T, P]) for i in range(2)]
        stage = sb("stage", [P, STAGE, N])
        ring = sb("ring", [P, RING, N])
        x_in = sb("x_in", [P, T, P])
        x_t = sb("x_t", [P, N])
        hi = {"Q": sb("q_hi", [P, N], F32R), "K": sb("k_hi", [P, N], F32R)}
        lo = {"Q": sb("q_lo", [P, N], F32R), "K": sb("k_lo", [P, N], F32R)}
        x_res = sb("x_res", [P, T, P])
        x_bo = sb("x_bo", [P, T, P])
        y = [sb(f"y{i}", [P, T, P]) for i in range(2)]
        b_rows = y[1][0:1, :, :].rearrange("p t f -> p (t f)")
        norm_row = sb("norm_row", [P, 2, HALF])
        scaled = sb("scaled", [P, 2, HALF])
        ctx_t = sb("ctx_t", [P, 2, HALF])
        w_t = sb("w_t", [P, 2, 4, P])
        b_cols = sb("b_cols", [P, 4])
        b_all = sb("b_all", [P, 6, P])
        ident = sb("ident", [P, P])
        ident_bf = sb("ident_bf", [P, P], BF16)
        ones = sb("ones", [P, P])
        row_max = sb("row_max", [P, 2, UNITS])
        row_sum = sb("row_sum", [P, 2, UNITS])
        inv_sum = sb("inv_sum", [P, 16])
        stats = sb("stats", [P, T, 6])
        moments = sb("moments", [P, T, 2])
        rstd = sb("rstd", [P, T])
        power = sb("power", [P, T])

        score = ctx.enter_context(nc.psum_tensor("score", [P, 2, N], F32))
        acc = ctx.enter_context(nc.psum_tensor("acc", [P, 3, HALF], F32))
        work = ctx.enter_context(nc.psum_tensor("work", [P, HALF], F32))

        consts_made = sem("consts_made")
        weights_loaded = sem("weights_loaded")
        rows_loaded = sem("rows_loaded")
        adj_loaded = [sem(f"adj_loaded{i}") for i in range(4)]
        weights_turned = sem("weights_turned")
        weights_placed = sem("weights_placed")
        bias_scaled = sem("bias_scaled")
        mask_biased = sem("mask_biased")
        mask_turned = sem("mask_turned")
        mask_clipped = sem("mask_clipped")
        xin_loaded = sem("xin_loaded")
        xres_loaded = sem("xres_loaded")
        q_stacked = sem("q_stacked")
        k_stacked = sem("k_stacked")
        stored = [sem(f"stored{i}") for i in range(2)]
        work_ready = sem("work_ready")
        work_read = sem("work_read")
        hi_ready = sem("hi_ready")
        xbo_ready = sem("xbo_ready")
        l0_scores = sem("l0_scores")
        l0_clipped = sem("l0_clipped")
        l0_exped = sem("l0_exped")
        l0_sums = sem("l0_sums")
        l0_ctx = sem("l0_ctx")
        l0_lned = sem("l0_lned")
        l0_inv = sem("l0_inv")
        l0_scaled = sem("l0_scaled")
        l0_summed = sem("l0_summed")
        l1_scores = sem("l1_scores")
        l1_masked = sem("l1_masked")
        l1_exped = sem("l1_exped")
        l1_turned = sem("l1_turned")
        l1_copied0 = sem("l1_copied0")
        l1_copied1 = sem("l1_copied1")
        l1_ctx = sem("l1_ctx")
        l1_recip = sem("l1_recip")
        l1_inv = sem("l1_inv")
        l1_expanded = sem("l1_expanded")
        l1_normed = sem("l1_normed")
        stats_made = sem("stats_made")
        moments_made = sem("moments_made")
        ln_steps = sem("ln_steps")

        waits_passed = {e: sem(f"waits_passed_{e}") for e in ("sp", "dve", "pool")}

        def ln_base(m):
            return 1 + (11 * m.b if m.layer == 0 else 11 * B + 4 * m.b)

        def moments_base(m):
            return 2 * m.b if m.layer == 0 else 2 * B + m.b

        def use(m, prev, nxt, name):
            return m.at + uses_of(m, prev, nxt).index(name) + 1

        def on_dve(u):
            return u % 4 != 3

        def walk(eng, body, prologue, epilogue):
            at0 = 8

            def batch(layer, par, b, turn):
                if layer == 0:
                    at = at0 if isinstance(b, int) and b == 0 else at0 - 1 + 10 * b
                else:
                    at = at0 - 1 + 10 * B if isinstance(b, int) and b == 0 else at0 - 2 + 10 * B + 12 * b
                return Batch(layer, par, b + B * layer, b, turn, isinstance(b, int) and b == 0, at)

            prologue(batch(0, 0, 0, 0))
            for layer in range(2):
                before = batch(0, 1, B - 1, B // 2 - 1) if layer else None
                body(batch(layer, 0, 0, 0), before, batch(layer, 1, 1, 0))
                with eng.Fori(0, (B - 2) // 2) as i:
                    odd, even = batch(layer, 1, 2 * i + 1, i), batch(layer, 0, 2 * i + 2, i + 1)
                    body(odd, batch(layer, 0, 2 * i, i), even)
                    body(even, odd, batch(layer, 1, 2 * i + 3, i + 1))
                last = batch(layer, 1, B - 1, B // 2 - 1)
                body(last, batch(layer, 0, B - 2, B // 2 - 1), batch(1, 0, 0, 0) if layer == 0 else None)
            epilogue(last)

        def setup_bank(i):
            return work[:, :] if i % 4 == 3 else acc[:, i % 4, :]

        def last_at():
            return 8 - 2 + 10 * B + 12 * (B - 1) + 4

        TAIL = range(UNITS, UNITS + 7)

        def at_once(m):
            return m.layer == 1 and m.first

        block = ctx.enter_context(nc.Block())

        @block.sync
        def _(sp):
            for half in stored:
                sp.sem_inc(half, DMA)
            w_in = x_t[:, :].rearrange("p (l m f) -> p l m f", l=2, m=4)
            for i, w in enumerate((wq0, wk0, wv0, wo0, wq1, wk1, wv1, wo1)):
                sp.dma_start(w_in[:, i // 4, i % 4, :], w).then_inc(weights_loaded, DMA)
            sp.dma_start(x_in[:, :, :], x_view[0]).then_inc(xin_loaded, DMA)
            adj_view = adj.rearrange("(t p) k -> p t k", p=P)
            adj_in = ring[:, :, :].bitcast(I32)
            for i, loaded in enumerate(adj_loaded):
                sp.dma_start(adj_in[:, 2 * i:2 * i + 2, :], adj_view[:, 2 * i:2 * i + 2, :]).then_inc(loaded, DMA)

            def stack(m, which, base, first_use):
                dst = (q_stack if which == "Q" else k_stack)[m.par]
                done = q_stacked if which == "Q" else k_stacked
                slots = (hi, hi, lo, lo) if which == "Q" else (hi, lo, hi, lo)
                wait_alone(sp, work_read, first_use + 1, waits_passed["sp"])
                if m.layer == 0:
                    wait_alone(sp, l0_scores, UNITS * (m.b - 1), waits_passed["sp"])
                else:
                    wait_alone(sp, l0_scores, UNITS * B - UNITS * (1 if m.first else 0), waits_passed["sp"])
                    wait_alone(sp, l1_scores, UNITS * (m.b - 1), waits_passed["sp"])
                for j, part in enumerate(slots):
                    for h in range(HEADS):
                        sp.dma_start(dst[HD * j:HD * j + HD, h, :].bitcast(F32),
                                     part[which][HD * h:HD * h + HD, :].bitcast(F32)).then_inc(done, DMA)

            def store(m):
                target = x1_view if m.layer == 0 else out_view
                wait_alone(sp, ln_steps, ln_base(m) + (11 if m.layer == 0 else 4), waits_passed["sp"])
                sp.dma_start(one(target, m.b), y[m.par][:, :, :]).then_inc(stored[m.par], DMA)

            def body(m, prev, nxt):
                if nxt is not None:
                    wait_alone(sp, hi_ready, 4 * m.g + 4, waits_passed["sp"])
                    if nxt.layer == 1:
                        wait_alone(sp, stored[nxt.par], DMA * (nxt.turn + 2), waits_passed["sp"])
                    source = x_view if nxt.layer == 0 else x1_view
                    sp.dma_start(x_in[:, :, :], one(source, nxt.b)).then_inc(xin_loaded, DMA)
                    stack(nxt, "Q", m, use(m, prev, nxt, "Q0"))
                    stack(nxt, "K", m, use(m, prev, nxt, "K0"))
                if prev is not None:
                    store(prev)

            def prologue(m):
                stack(m, "Q", m, 3)
                stack(m, "K", m, 5)

            def epilogue(m):
                store(m)
                for half in stored:
                    sp.wait_ge(half, DMA * (B + 1))

            walk(sp, body, prologue, epilogue)

        @block.tensor
        def _(pe):
            def fill(n):
                wait(pe, work_read, n - 1)

            def turn_tile(out, tile):
                return pe.transpose(out, tile, ident[:, :])

            def turn_weights(layer):
                for m in range(4):
                    mm = turn_tile(score[:, 0, layer * HALF + m * P:layer * HALF + (m + 1) * P],
                                   x_t[:, (layer * 4 + m) * P:(layer * 4 + m + 1) * P])
                mm.then_inc(weights_turned, 1)

            def spread_rows():
                pe.wait_ge(rows_loaded, DMA * 10)
                for i, (a, b) in enumerate(((0, 4), (4, 6))):
                    pe.matmul(score[:, 1, i * HALF:i * HALF + (b - a) * P], ones[0:1, :], b_rows[0:1, a * P:b * P],
                              start=True, stop=True).then_inc(weights_turned, 1)

            def prep(m, name, n, bank=work[:, :]):
                half = int(name[1])
                cols = slice(half * HALF, (half + 1) * HALF)
                if m.layer == 0 and m.first:
                    wait(pe, work_read, n - 4)
                else:
                    fill(n)
                if name[0] == "X":
                    if half == 0:
                        pe.wait_ge(xin_loaded, DMA * (m.g + 1))
                    for t in range(4):
                        mm = turn_tile(bank[:, t * P:(t + 1) * P], x_in[:, 4 * half + t, :])
                elif name[0] == "V":
                    for t in range(4):
                        mm = pe.matmul(bank[:, t * P:(t + 1) * P], x_t[:, (4 * half + t) * P:(4 * half + t + 1) * P],
                                       w_t[:, m.layer, 2, :], start=True, stop=True)
                else:
                    mm = pe.matmul(bank, w_t[:, m.layer, "QK".index(name[0]), :], x_t[:, cols],
                                   start=True, stop=True)
                mm.then_inc(work_ready, 1)

            def project(m, half, n):
                fill(n)
                if m.layer == 0:
                    pe.wait_ge(l0_summed, 14 * m.b + 7 * (half + 1))
                else:
                    pe.wait_ge(l1_normed, 2 * m.b + half + 1)
                for t in range(4):
                    mm = pe.matmul(work[:, t * P:(t + 1) * P], ctx_t[:, half, t * P:(t + 1) * P],
                                   w_t[:, m.layer, 3, :], start=True, stop=True)
                mm.then_inc(work_ready, 1)

            def turn_inverse(m, half, n):
                fill(n)
                pe.wait_ge(l1_expanded, 2 * m.b + half + 1)
                for t in range(4):
                    mm = turn_tile(work[:, t * P:(t + 1) * P], norm_row[:, 0, t * P:(t + 1) * P])
                mm.then_inc(work_ready, 1)

            def scores(m, u):
                if u == 0:
                    pe.wait_ge(q_stacked, DMA * STACK_DMAS * (m.g + 1))
                    pe.wait_ge(k_stacked, DMA * STACK_DMAS * (m.g + 1))
                    if m.layer == 0 and m.first:
                        pe.wait_ge(mask_clipped, T)
                    if m.layer == 1 and m.first:
                        pe.wait_ge(l0_clipped, UNITS * B)
                qs, ks = q_stack[m.par], k_stack[m.par]
                if m.layer == 0:
                    wait(pe, l0_clipped, UNITS * m.b + u - 1)
                    half, kt, hp = u // 16, u // 2 % 8, u % 2
                    for i in range(2):
                        h = 2 * hp + i
                        mm = pe.matmul(score[:, u % 2, i * HALF:(i + 1) * HALF], ks[:, h, kt * P:(kt + 1) * P],
                                       qs[:, h, half * HALF:(half + 1) * HALF], start=True, stop=True)
                    mm.then_inc(l0_scores, 1)
                else:
                    wait(pe, l1_masked, UNITS * m.b + u - 1)
                    qt, h = u // 4, u % 4
                    for i in range(2):
                        mm = pe.matmul(score[:, u % 2, i * HALF:(i + 1) * HALF], qs[:, h, qt * P:(qt + 1) * P],
                                       ks[:, h, i * HALF:(i + 1) * HALF], start=True, stop=True)
                    mm.then_inc(l1_scores, 1)

            def pair(m, p):
                pe.wait_ge(l0_exped, UNITS * m.b + 2 * p + 2)
                for what in range(2):
                    if (what == 0) == (p == 0):
                        wait(pe, l0_lned, PAIRS * m.b + p)
                    else:
                        wait(pe, l0_scaled, PAIRS * m.b + (p - 1 if p else 0))
                    bank = (2 * p + what) % 3
                    for h in range(HEADS):
                        u = 2 * p + h // 2
                        w = v_tok[m.par][:, p % 8, HD * h:HD * h + HD] if what else ones[:, 0:HD]
                        mm = pe.matmul(acc[HD * h:HD * h + HD, bank, :], w,
                                       ring[:, u % RING, (h % 2) * HALF:(h % 2 + 1) * HALF],
                                       start=True, stop=True)
                    mm.then_inc(l0_ctx if what else l0_sums, 1)

            def turn(m, u):
                pe.wait_ge(l1_exped, UNITS * m.b + u + 1)
                if m.first and u == 0:
                    pe.wait_ge(l0_lned, PAIRS * B)
                    pe.wait_ge(l0_scaled, PAIRS * B)
                for c in range(2):
                    wait(pe, (l1_copied0, l1_copied1)[c], UNITS * m.b + u)
                    for t in range(4):
                        mm = turn_tile(acc[:, c, t * P:(t + 1) * P],
                                       stage[:, u % STAGE, (4 * c + t) * P:(4 * c + t + 1) * P])
                    mm.then_inc(l1_turned, 1)

            def context(m, qt, part):
                if part == 0:
                    pe.wait_ge(l1_copied0, UNITS * m.b + 4 * qt + 4)
                    pe.wait_ge(l1_copied1, UNITS * m.b + 4 * qt + 4)
                    if qt % 4 == 0:
                        wait(pe, l1_normed, 2 * m.b + qt // 4)
                for kt in ((0, 1, 2), (3, 4, 5), (6, 7))[part]:
                    for h in range(HEADS):
                        mm = pe.matmul(acc[HD * h:HD * h + HD, 2, (qt % 4) * P:(qt % 4 + 1) * P],
                                       v_tok[m.par][:, kt, HD * h:HD * h + HD],
                                       ring[:, (4 * qt + h) % RING, kt * P:(kt + 1) * P],
                                       start=(kt == 0), stop=(kt == T - 1))
                if part == 2:
                    mm.then_inc(l1_ctx, 1)

            def attend(m, s):
                if m.layer == 0:
                    if s % 2 and 5 <= s <= 35:
                        pair(m, (s - 5) // 2)
                else:
                    if 3 <= s < UNITS + 3:
                        turn(m, s - 3)
                    if 7 <= s < UNITS + 6 and (s - 7) % 4 < 3:
                        context(m, (s - 7) // 4, (s - 7) % 4)

            PREP_AT = {10: "X0", 11: "X1", 12: "Q0", 14: "Q1", 16: "K0", 18: "K1", 22: "V0", 24: "V1"}

            def body(m, prev, nxt):
                if at_once(m):
                    for s in TAIL:
                        attend(prev, s)
                for s in range(UNITS):
                    scores(m, s)
                    if prev is not None:
                        if not at_once(m):
                            attend(prev, s + UNITS)
                        if prev.layer and s == 5:
                            turn_inverse(prev, 1, use(m, prev, nxt, "R1"))
                        if s == 8:
                            project(prev, 1, use(m, prev, nxt, "Wo1"))
                    attend(m, s)
                    if nxt is not None and s in PREP_AT:
                        prep(nxt, PREP_AT[s], use(m, prev, nxt, PREP_AT[s]))
                    if m.layer and s == 20:
                        turn_inverse(m, 0, use(m, prev, nxt, "R0"))
                    if s == 27:
                        project(m, 0, use(m, prev, nxt, "Wo0"))

            def prologue(m):
                pe.wait_ge(consts_made, 5)
                pe.wait_ge(weights_loaded, DMA * 8)
                turn_weights(0)
                turn_weights(1)
                for i, name in enumerate(("X0", "X1", "Q0", "Q1", "K0", "K1", "V0", "V1")):
                    if name == "Q0":
                        pe.wait_ge(weights_placed, 1)
                        pe.wait_ge(work_read, 2)
                    prep(m, name, i + 1, setup_bank(i))
                spread_rows()
                score_bf = score[:, :, :].bitcast(BF16).rearrange("p a (c n) -> p (a c) n", c=2)
                pe.wait_ge(mask_biased, T)
                pe.wait_ge(weights_placed, 4)
                for kt in range(T):
                    wait(pe, mask_clipped, kt - 3)
                    for qt in range(T):
                        mm = pe.transpose(score_bf[:, kt % 4, qt * P:(qt + 1) * P],
                                          bias_mask[:, qt, kt * P:(kt + 1) * P], ident_bf[:, :])
                    mm.then_inc(mask_turned, 1)

            def epilogue(m):
                for s in range(UNITS, UNITS + 6):
                    attend(m, s)
                turn_inverse(m, 1, last_at() + 1)
                project(m, 1, last_at() + 2)

            walk(pe, body, prologue, epilogue)

        @block.vector
        def _(dve):
            def place_weights(layer):
                dve.wait_ge(weights_turned, layer + 1)
                turned = score[:, 0, layer * HALF:(layer + 1) * HALF]
                dve.tensor_scalar(w_t[:, layer, 0, :], turned[:, 0:P], SCALE, None, ALU.mult)
                dve.tensor_copy(w_t[:, layer, 1:4, :],
                                turned[:, P:4 * P].rearrange("p (m f) -> p m f", m=3)).then_inc(weights_placed, 1)

            def place_rows():
                for i, (a, b) in enumerate(((0, 4), (4, 6))):
                    dve.wait_ge(weights_turned, 3 + i)
                    dve.tensor_copy(b_all[:, a:b, :],
                                    score[:, 1, i * HALF:i * HALF + (b - a) * P].rearrange("p (m f) -> p m f", f=P))\
                       .then_inc(weights_placed, 1)

            adj_in = ring[:, :, :].bitcast(I32)
            score_bf = score[:, :, :].bitcast(BF16).rearrange("p a (c n) -> p (a c) n", c=2)

            def bias_masks():
                for t in range(T):
                    if t % 2 == 0:
                        dve.wait_ge(adj_loaded[t // 2], DMA)
                    dve.tensor_scalar(bias_mask[:, t, :], adj_in[:, t, :], 0.0, MASKED, ALU.is_equal, ALU.mult)\
                       .then_inc(mask_biased, 1)

            def clip_masks():
                for kt in range(T):
                    dve.wait_ge(mask_turned, kt + 1)
                    dve.tensor_scalar(clip_mask[:, kt, :], score_bf[:, kt % 4, :], -2 * CLIP, CLIP,
                                      ALU.max, ALU.add).then_inc(mask_clipped, 1)

            def low_part(m, name, n, bank=work[:, :]):
                which, half = name[0], int(name[1])
                cols = slice(half * HALF, (half + 1) * HALF)
                k = ("Q0", "Q1", "K0", "K1").index(name)
                dve.wait_ge(hi_ready, 4 * m.g + k + 1)
                c = 2 * m.layer + "QK".index(which)
                dve.scalar_tensor_tensor(out=lo[which][:, cols], in0=bank, scalar=b_cols[:, c:c + 1],
                                         in1=hi[which][:, cols].bitcast(F32), op0=ALU.add, op1=ALU.subtract)\
                   .then_inc(work_read, 1)

            def take_v(m, half, n, bank=work[:, :]):
                dve.wait_ge(work_ready, n)
                if m.layer == 0:
                    wait(dve, l0_ctx, PAIRS * (m.b - 1))
                else:
                    dve.wait_ge(l0_ctx, PAIRS * B - PAIRS * (1 if m.first else 0))
                    wait(dve, l1_ctx, T * (m.b - 1))
                dve.tensor_tensor(v_tok[m.par][:, 4 * half:4 * half + 4, :],
                                  bank.rearrange("p (t f) -> p t f", t=4),
                                  b_all[:, 2 + m.layer, :][:, None, :].to_broadcast([P, 4, P]), ALU.add)\
                   .then_inc(work_read, 1)

            def clip(m, u):
                dve.wait_ge(l0_scores, UNITS * m.b + u + 1)
                wait(dve, l0_exped, UNITS * m.b + u - STAGE + 1)
                half, kt = u // 16, u // 2 % 8
                dve.scalar_tensor_tensor(
                    out=stage[:, u % STAGE, :].rearrange("p (h n) -> p h n", h=2),
                    in0=score[:, u % 2, :].rearrange("p (h n) -> p h n", h=2), scalar=-CLIP,
                    in1=clip_mask[:, kt, half * HALF:(half + 1) * HALF][:, None, :].to_broadcast([P, 2, HALF]),
                    op0=ALU.max, op1=ALU.min).then_inc(l0_clipped, 1)

            def scale_pair(m, p):
                dve.wait_ge(l0_ctx, PAIRS * m.b + p + 1)
                dve.wait_ge(l0_inv, PAIRS * m.b + p + 1)
                half, kt = p // 8, p % 8
                if kt == 0:
                    target = ctx_t[:, half, :]
                else:
                    target = scaled[:, p % 2, :]
                    adds = 7 * half + kt - 1
                    wait(dve, l0_summed, 14 * m.b + adds - (1 if kt > 1 else 0))
                dve.tensor_tensor(target, acc[:, (2 * p + 1) % 3, :], norm_row[:, p % 2, :], ALU.mult)\
                   .then_inc(l0_scaled, 1)

            def mask_max(m, u):
                dve.wait_ge(l1_scores, UNITS * m.b + u + 1)
                wait_alone(dve, l1_turned, 2 * (UNITS * m.b + u - STAGE + 1), waits_passed["dve"])
                if m.first and u == 0:
                    dve.wait_ge(l0_exped, UNITS * B)
                dve.tensor_tensor_reduce(
                    out=stage[:, u % STAGE, :], in0=score[:, u % 2, :], in1=bias_mask[:, u // 4, :],
                    scale=-1.0, scalar=3e38, op0=ALU.add, op1=ALU.min,
                    accum_out=row_max[:, m.par, u:u + 1]).then_inc(l1_masked, 1)

            def copy_turned(m, u):
                dve.wait_ge(l1_turned, 2 * (UNITS * m.b + u + 1))
                wait(dve, l1_ctx, T * m.b + u // 4 - 1)
                dve.tensor_copy(ring[:, u % RING, HALF:N], acc[:, 1, :]).then_inc(l1_copied1, 1)

            def invert(m, half):
                dve.wait_ge(l1_exped, UNITS * m.b + 16 * (half + 1))
                wait(dve, l1_expanded, 2 * m.b + half)
                units = slice(16 * half, 16 * half + 16)
                dve.reciprocal(inv_sum[:, :], row_sum[:, m.par, units]).then_inc(l1_recip, 1)
                dve.wait_ge(l1_recip, 4 * m.b + 2 * half + 1)
                dve.scalar_tensor_tensor(out=inv_sum[:, :], in0=row_max[:, m.par, units], scalar=-0.5 * MASKED,
                                         in1=inv_sum[:, :], op0=ALU.is_lt, op1=ALU.mult).then_inc(l1_recip, 1)

            def normalise(m, half, n):
                dve.wait_ge(l1_ctx, T * m.b + 4 * (half + 1))
                dve.wait_ge(work_read, n)
                dve.tensor_tensor(ctx_t[:, half, :], acc[:, 2, :], norm_row[:, 1, :], ALU.mult).then_inc(l1_normed, 1)

            def add_residual(m, half, n):
                dve.wait_ge(work_ready, n)
                if half == 0:
                    dve.wait_ge(xbo_ready, m.g + 1)
                    wait(dve, stored[m.par], DMA * (m.turn + B // 2 * m.layer + 1))
                dve.tensor_tensor(y[m.par][:, 4 * half:4 * half + 4, :],
                                  work[:, :].rearrange("p (t f) -> p t f", t=4),
                                  x_bo[:, 4 * half:4 * half + 4, :], ALU.add).then_inc(work_read, 1)

            def layer_stats(m, which, n):
                if which == 0:
                    dve.wait_ge(work_read, n)
                    wait(dve, ln_steps, ln_base(m))
                else:
                    dve.wait_ge(ln_steps, ln_base(m) + 7)
                base = moments_base(m) + which
                for t in range(T):
                    dve.bn_stats(stats[:, t, :], y[m.par][:, t, :]).then_inc(stats_made, 1)
                wait_alone(dve, stats_made, T * (base + 1), waits_passed["dve"])
                for t in range(T):
                    mm = dve.bn_aggr(moments[:, t, :], stats[:, t, :])
                mm.then_inc(moments_made, 1)

            def attend(m, s, n_r=(None, None)):
                if m.layer == 0:
                    if s % 2 == 0 and 6 <= s <= 36:
                        scale_pair(m, (s - 6) // 2)
                else:
                    if 2 <= s < UNITS + 2 and on_dve(s - 2):
                        copy_turned(m, s - 2)

            LOW_AT = {12: "Q0", 14: "Q1", 16: "K0", 18: "K1"}
            V_AT = {22: 0, 24: 1}

            def body(m, prev, nxt):
                if at_once(m):
                    for s in TAIL:
                        attend(prev, s)
                for s in range(UNITS):
                    (mask_max if m.layer else clip)(m, s)
                    if prev is not None:
                        if not at_once(m):
                            attend(prev, s + UNITS)
                        if prev.layer and s == 1:
                            invert(prev, 1)
                        if prev.layer and s == 5:
                            normalise(prev, 1, use(m, prev, nxt, "R1"))
                        if s == 8:
                            add_residual(prev, 1, use(m, prev, nxt, "Wo1"))
                        if s == 9:
                            layer_stats(prev, 0, use(m, prev, nxt, "Wo1"))
                        if prev.layer == 0 and s == 24:
                            layer_stats(prev, 1, None)
                    if nxt is not None:
                        if s in LOW_AT:
                            low_part(nxt, LOW_AT[s], use(m, prev, nxt, LOW_AT[s]))
                        if s in V_AT:
                            take_v(nxt, V_AT[s], use(m, prev, nxt, f"V{V_AT[s]}"))
                    if m.layer and s == 17:
                        invert(m, 0)
                    if m.layer and s == 21:
                        normalise(m, 0, use(m, prev, nxt, "R0"))
                    if s == 27:
                        add_residual(m, 0, use(m, prev, nxt, "Wo0"))
                    attend(m, s)

            def prologue(m):
                place_weights(0)
                dve.wait_ge(rows_loaded, DMA * 10)
                dve.tensor_scalar(b_cols[:, 0:4:2], b_cols[:, 0:4:2], SCALE, None, ALU.mult).then_inc(bias_scaled, 1)
                place_weights(1)
                for i, name in enumerate(("Q0", "Q1", "K0", "K1")):
                    low_part(m, name, 3 + i, setup_bank(2 + i))
                place_rows()
                dve.wait_ge(weights_placed, 4)
                for half in range(2):
                    take_v(m, half, 7 + half, setup_bank(6 + half))
                bias_masks()
                clip_masks()

            def epilogue(m):
                for s in range(UNITS, UNITS + 2):
                    attend(m, s)
                invert(m, 1)
                normalise(m, 1, last_at() + 1)
                add_residual(m, 1, last_at() + 2)
                layer_stats(m, 0, last_at() + 2)

            walk(dve, body, prologue, epilogue)

        @block.scalar
        def _(act):
            for i, v in enumerate((bq0, bk0, bq1, bk1)):
                act.dma_start(b_cols[:, i:i + 1], v.rearrange("(d a) -> d a", a=1)).then_inc(rows_loaded, DMA)
            for i, v in enumerate((bo0, bo1, bv0, bv1, gamma, beta)):
                act.dma_start(b_rows[0:1, i * P:(i + 1) * P], v.rearrange("(a d) -> a d", a=1)).then_inc(rows_loaded, DMA)
            act.preload_act_table_set("natural_log_exp_and_others")

            def take_x(half, n, bank=work[:, :]):
                act.wait_ge(work_ready, n)
                act.activation(x_t[:, half * HALF:(half + 1) * HALF], bank, ACT.Copy).then_inc(work_read, 1)

            def high_part(m, name, n, bank=work[:, :]):
                which, half = name[0], int(name[1])
                act.wait_ge(work_ready, n)
                wait(act, q_stacked if which == "Q" else k_stacked, DMA * STACK_DMAS * m.g)
                c = 2 * m.layer + "QK".index(which)
                act.activation(hi[which][:, half * HALF:(half + 1) * HALF], bank, ACT.Identity,
                               bias=b_cols[:, c:c + 1]).then_inc(hi_ready, 1)

            def exp0(m, u):
                act.wait_ge(l0_clipped, UNITS * m.b + u + 1)
                wait(act, l0_ctx, PAIRS * m.b + u // 2 - 3)
                act.activation(ring[:, u % RING, :], stage[:, u % STAGE, :], ACT.Exp).then_inc(l0_exped, 1)

            def log_sums(m, p):
                act.wait_ge(l0_sums, PAIRS * m.b + p + 1)
                wait(act, l0_scaled, PAIRS * m.b + p - 1)
                act.activation(norm_row[:, p % 2, :], acc[:, (2 * p) % 3, :], ACT.Ln).then_inc(l0_lned, 1)

            def inverse_sums(m, p):
                act.wait_ge(l0_lned, PAIRS * m.b + p + 1)
                act.activation(norm_row[:, p % 2, :], norm_row[:, p % 2, :], ACT.Exp, scale=-1.0).then_inc(l0_inv, 1)

            def exp1(m, u):
                act.wait_ge(l1_masked, UNITS * m.b + u + 1)
                act.activation(stage[:, u % STAGE, :], stage[:, u % STAGE, :], ACT.Exp,
                               bias=row_max[:, m.par, u:u + 1], scale=-1.0,
                               accum_out=row_sum[:, m.par, u:u + 1]).then_inc(l1_exped, 1)

            def copy_turned(m, u, c):
                act.wait_ge(l1_turned, 2 * (UNITS * m.b + u) + c + 1)
                wait(act, l1_ctx, T * m.b + u // 4 - 1)
                act.activation(ring[:, u % RING, c * HALF:(c + 1) * HALF], acc[:, c, :], ACT.Copy)\
                   .then_inc((l1_copied0, l1_copied1)[c], 1)

            def take_inverse(m, half, n):
                act.wait_ge(work_ready, n)
                wait(act, l1_normed, 2 * m.b + half)
                act.activation(norm_row[:, 1, :], work[:, :], ACT.Copy).then_inc(work_read, 1)

            def attend(m, s):
                if m.layer == 1 and 1 <= s < UNITS + 1:
                    copy_turned(m, s - 1, 0)
                    if not on_dve(s - 1):
                        copy_turned(m, s - 1, 1)

            def pair_before(m, s):
                if m is not None and m.layer == 0 and s % 2 == 0 and 4 <= s <= 34:
                    log_sums(m, (s - 4) // 2)

            def pair_after(m, s):
                if m is not None and m.layer == 0 and s % 2 == 0 and 4 <= s <= 34:
                    inverse_sums(m, (s - 4) // 2)

            def body(m, prev, nxt):
                if at_once(m):
                    for s in TAIL:
                        pair_before(prev, s)
                        pair_after(prev, s)
                for s in range(UNITS):
                    if not at_once(m):
                        pair_before(prev, s + UNITS)
                    pair_before(m, s)
                    if prev is not None and prev.layer and s == 4:
                        take_inverse(prev, 1, use(m, prev, nxt, "R1"))
                    if nxt is not None:
                        if s in (9, 10):
                            take_x(s - 9, use(m, prev, nxt, f"X{s - 9}"))
                        if s in (11, 13, 15, 17):
                            name = {11: "Q0", 13: "Q1", 15: "K0", 17: "K1"}[s]
                            high_part(nxt, name, use(m, prev, nxt, name))
                    if m.layer and s == 19:
                        take_inverse(m, 0, use(m, prev, nxt, "R0"))
                    (exp1 if m.layer else exp0)(m, s)
                    if not at_once(m):
                        pair_after(prev, s + UNITS)
                    pair_after(m, s)
                    if prev is not None:
                        attend(prev, s + UNITS)
                    attend(m, s)

            def prologue(m):
                act.wait_ge(weights_turned, 2)
                for half in range(2):
                    take_x(half, 1 + half, setup_bank(half))
                act.wait_ge(bias_scaled, 1)
                for i, name in enumerate(("Q0", "Q1", "K0", "K1")):
                    high_part(m, name, 3 + i, setup_bank(2 + i))
                act.wait_ge(mask_biased, T)

            def epilogue(m):
                attend(m, UNITS)
                take_inverse(m, 1, last_at() + 1)

            walk(act, body, prologue, epilogue)

        @block.gpsimd
        def _(pool):
            pool.memset(ident[:, :], 0.0).then_inc(consts_made, 1)
            pool.memset(ones[:, :], 1.0).then_inc(consts_made, 1)
            pool.memset(power[:, :], -0.5).then_inc(consts_made, 1)
            pool.wait_ge(consts_made, 3)
            pool.affine_select(out=ident[:, :], in_=ident[:, :], compare_op=ALU.not_equal, fill=1.0, base=0,
                               pattern=[[-1, P]], channel_multiplier=1).then_inc(consts_made, 1)
            pool.wait_ge(consts_made, 4)
            pool.tensor_copy(ident_bf[:, :], ident[:, :]).then_inc(consts_made, 1)
            pool.sem_inc(ln_steps, 1)

            def spread(row):
                return row[:, None, :].to_broadcast([P, T, P])

            def per_token(col):
                return col[:, :, None].to_broadcast([P, T, P])

            def load_residual(m, prev):
                if m.layer == 1:
                    wait_alone(pool, stored[m.par], DMA * (m.turn + 2), waits_passed["pool"])
                source = x_view if m.layer == 0 else x1_view
                if prev is not None:
                    wait_alone(pool, xbo_ready, m.g, waits_passed["pool"])
                    if prev.layer == 0:
                        wait_alone(pool, ln_steps, ln_base(prev) + 7, waits_passed["pool"])
                pool.dma_start(x_res[:, :, :], one(source, m.b)).then_inc(xres_loaded, DMA)

            def add_bias(m, prev, n_free):
                pool.wait_ge(xres_loaded, DMA * (m.g + 1))
                if prev is not None:
                    pool.wait_ge(work_read, n_free)
                else:
                    pool.wait_ge(weights_placed, 3)
                pool.tensor_tensor(x_bo[:, :, :], x_res[:, :, :], spread(b_all[:, m.layer, :]), ALU.add)\
                    .then_inc(xbo_ready, 1)

            def step(op, m, k):
                if k > 1:
                    wait_alone(pool, ln_steps, ln_base(m) + k - 1, waits_passed["pool"])
                op().then_inc(ln_steps, 1)

            def normalise_tokens(m, k):
                which, k0 = (0, 0) if k < 8 else (1, 7)
                if k == k0 + 1:
                    wait_alone(pool, moments_made, moments_base(m) + which + 1, waits_passed["pool"])
                yt = y[m.par][:, :, :]
                if k == k0 + 1:
                    step(lambda: pool.tensor_scalar(rstd[:, :], moments[:, :, 1], EPS, 1.0, ALU.add, ALU.mult), m, k)
                elif k == k0 + 2:
                    step(lambda: pool.tensor_tensor(rstd[:, :], rstd[:, :], power[:, :], ALU.pow), m, k)
                elif k == k0 + 3:
                    step(lambda: pool.tensor_tensor(yt, yt, per_token(moments[:, :, 0]), ALU.subtract), m, k)
                elif k == k0 + 4:
                    step(lambda: pool.tensor_tensor(yt, yt, per_token(rstd[:, :]), ALU.mult), m, k)

            def affine_residual(m, k):
                yt = y[m.par][:, :, :]
                other = {5: spread(b_all[:, 4, :]), 6: spread(b_all[:, 5, :]), 7: x_res[:, :, :]}[k]
                step(lambda: pool.tensor_tensor(yt, yt, other, ALU.mult if k == 5 else ALU.add), m, k)

            def sum_pair(m, p):
                half, kt = p // 8, p % 8
                pool.wait_ge(l0_scaled, PAIRS * m.b + p + 1)
                if kt:
                    wait(pool, l0_summed, 14 * m.b + 7 * half + kt - 1)
                    pool.tensor_tensor(ctx_t[:, half, :], ctx_t[:, half, :], scaled[:, p % 2, :], ALU.add)\
                        .then_inc(l0_summed, 1)

            def expand(m, half, n_free):
                pool.wait_ge(l1_recip, 4 * m.b + 2 * half + 2)
                if m.first and half == 0:
                    pool.wait_ge(l0_scaled, PAIRS * B)
                elif n_free is not None:
                    pool.wait_ge(work_ready, n_free)
                pool.tensor_tensor(norm_row[:, 0, :].rearrange("p (u d) -> p u d", d=HD),
                                   inv_sum[:, :, None].to_broadcast([P, 16, HD]),
                                   ones[:, 0:1][:, :, None].to_broadcast([P, 16, HD]), ALU.mult).then_inc(l1_expanded, 1)

            def attend(m, s):
                if m.layer == 0 and s % 2 == 0 and 8 <= s <= 38:
                    sum_pair(m, (s - 8) // 2)

            LN_AT = ({11: (1, 2, 3), 13: (4,), 15: (5,), 17: (6,), 19: (7,), 25: (8, 9, 10), 27: (11,)},
                     {11: (1, 2, 3), 13: (4,)})

            def body(m, prev, nxt):
                if at_once(m):
                    for s in TAIL:
                        attend(prev, s)
                for s in range(UNITS):
                    if prev is not None:
                        if not at_once(m):
                            attend(prev, s + UNITS)
                        if prev.layer and s == 2:
                            expand(prev, 1, prev.at + uses_of(prev, prev, m).index("R0") + 1 - (1 if prev.first else 0))
                    attend(m, s)
                    if prev is not None:
                        for k in LN_AT[prev.layer].get(s, ()):
                            (affine_residual if 5 <= k <= 7 else normalise_tokens)(prev, k)
                    if s == 20:
                        load_residual(m, prev)
                    if m.layer and s == 18:
                        expand(m, 0, use(m, prev, nxt, "R1") if prev.layer else None)
                    if s == 23:
                        add_bias(m, prev, use(m, prev, nxt, "Wo1") if prev is not None else None)

            def prologue(m):
                pass

            def epilogue(m):
                expand(m, 1, m.at + 3)
                for k in range(1, 5):
                    normalise_tokens(m, k)

            walk(pool, body, prologue, epilogue)


_INS = ["x", "adj"] + [f"L0_gnn_{n}" for n in ("Wq", "bq", "Wk", "bk", "Wv", "bv", "Wo", "bo", "gamma", "beta")] \
    + [f"L1_gnn_{n}" for n in ("wq", "bq", "wk", "bk", "wv", "bv", "wo", "bo")]


def kernel(**inputs):
    import numpy as _np
    import concourse.bacc as _bacc
    from concourse import mybir as _mybir
    from concourse.bass_utils import run_bass_kernel_spmd as _run

    nc = _bacc.Bacc("TRN2", target_bir_lowering=False, num_devices=1)
    arrays, args = {}, []
    for name in _INS:
        a = _np.ascontiguousarray(inputs[name])
        arrays[f"in_{name}"] = a
        args.append(nc.dram_tensor(f"in_{name}", a.shape, _mybir.dt.from_np(a.dtype), kind="ExternalInput").ap())
    shape = tuple(inputs["x"].shape)
    out = nc.dram_tensor("out_0", shape, _mybir.dt.float32, kind="ExternalOutput").ap()
    x1 = nc.dram_tensor("x1_scratch", shape, _mybir.dt.float32, kind="Internal").ap()
    adj_block_kernel(nc, *args, out, x1)
    r = _run(nc, [arrays], core_ids=[0])
    return r.results[0]["out_0"]
```

```python
from collections import namedtuple
from contextlib import ExitStack

import concourse.bass as bass
from concourse import mybir

F32 = mybir.dt.float32
F32R = mybir.dt.float32r
BF16 = mybir.dt.bfloat16
I8 = mybir.dt.int8
I32 = mybir.dt.int32
ALU = mybir.AluOpType
ACT = mybir.ActivationFunctionType

P = 128
HEADS = 4
HD = P // HEADS
RING = 8
STAGE = 4
CLIP = 10.0
MASKED = -2.0 ** 100
EPS = 1e-5
UNITS = 32
PAIRS = 16
DMA = 16
STACK_DMAS = 16
FIRST_USES = 8

Batch = namedtuple("Batch", "layer par g b turn first at")


def uses_of(batch, prev, nxt):
    order = []
    if prev is not None:
        order += (["R1"] if prev.layer else []) + ["Wo1"]
    if nxt is not None:
        order += ["X0", "X1", "Q0", "Q1", "K0", "K1"]
    if batch is not None and batch.layer:
        order += ["R0"]
    if nxt is not None:
        order += ["V0", "V1"]
    if batch is not None:
        order += ["Wo0"]
    return order


def wait(eng, sem, n):
    if isinstance(n, int) and n <= 0:
        return
    eng.wait_ge(sem, n)


def wait_alone(eng, sem, n, passed):
    wait(eng, sem, n)
    if not isinstance(n, int):
        eng.sem_inc(passed, 1)


def adj_block_kernel(
    nc, x, adj, wq0, bq0, wk0, bk0, wv0, bv0, wo0, bo0, gamma, beta,
    wq1, bq1, wk1, bk1, wv1, bv1, wo1, bo1, out, x1_dram,
):
    B, N, F = x.shape
    T = N // P
    assert F == P and T == 8 and B == 8
    SCALE = float(HD) ** -0.5
    HALF = N // 2

    x_view = x.rearrange("b (t p) f -> b p t f", p=P)
    x1_view = x1_dram.rearrange("b (t p) f -> b p t f", p=P)
    out_view = out.rearrange("b (t p) f -> b p t f", p=P)

    def one(view, b):
        return view[bass.ds(b, 1)].rearrange("o p t f -> (o p) t f")

    with ExitStack() as ctx:
        def sb(name, shape, dt=F32):
            return ctx.enter_context(nc.sbuf_tensor(name, shape, dt))

        def sem(name):
            return ctx.enter_context(nc.semaphore(name))

        clip_mask = sb("clip_mask", [P, T, N], I8)
        bias_mask = sb("bias_mask", [P, T, N], BF16)
        q_stack = [sb(f"q_stack{i}", [P, HEADS, N], F32R) for i in range(2)]
        k_stack = [sb(f"k_stack{i}", [P, HEADS, N], F32R) for i in range(2)]
        v_tok = [sb(f"v_tok{i}", [P, T, P]) for i in range(2)]
        stage = sb("stage", [P, STAGE, N])
        ring = sb("ring", [P, RING, N])
        x_in = sb("x_in", [P, T, P])
        x_t = sb("x_t", [P, N])
        hi = {"Q": sb("q_hi", [P, N], F32R), "K": sb("k_hi", [P, N], F32R)}
        lo = {"Q": sb("q_lo", [P, N], F32R), "K": sb("k_lo", [P, N], F32R)}
        x_res = sb("x_res", [P, T, P])
        x_bo = sb("x_bo", [P, T, P])
        y = [sb(f"y{i}", [P, T, P]) for i in range(2)]
        b_rows = y[1][0:1, :, :].rearrange("p t f -> p (t f)")
        norm_row = sb("norm_row", [P, 2, HALF])
        scaled = sb("scaled", [P, 2, HALF])
        ctx_t = sb("ctx_t", [P, 2, HALF])
        w_t = sb("w_t", [P, 2, 4, P])
        b_cols = sb("b_cols", [P, 5])
        b_all = sb("b_all", [P, 6, P])
        ident = sb("ident", [P, P])
        ident_bf = sb("ident_bf", [P, P], BF16)
        ones = sb("ones", [P, P])
        row_max = sb("row_max", [P, 2, UNITS])
        row_sum = sb("row_sum", [P, 2, UNITS])
        inv_sum = sb("inv_sum", [P, 16])
        stats = sb("stats", [P, T, 6])
        moments = sb("moments", [P, T, 2])
        rstd = sb("rstd", [P, T])
        power = sb("power", [P, T])

        score = ctx.enter_context(nc.psum_tensor("score", [P, 2, N], F32))
        acc = ctx.enter_context(nc.psum_tensor("acc", [P, 3, HALF], F32))
        work = ctx.enter_context(nc.psum_tensor("work", [P, HALF], F32))

        consts_made = sem("consts_made")
        weights_loaded = sem("weights_loaded")
        rows_loaded = sem("rows_loaded")
        adj_loaded = [sem(f"adj_loaded{i}") for i in range(4)]
        weights_turned = sem("weights_turned")
        weights_placed = sem("weights_placed")
        bias_scaled = sem("bias_scaled")
        mask_biased = sem("mask_biased")
        mask_turned = sem("mask_turned")
        mask_clipped = [sem(f"mask_clipped{i}") for i in range(2)]
        xin_loaded = sem("xin_loaded")
        xres_loaded = sem("xres_loaded")
        q_stacked = sem("q_stacked")
        k_stacked = sem("k_stacked")
        first_k_stacked = sem("first_k_stacked")
        stored = [sem(f"stored{i}") for i in range(2)]
        work_ready = sem("work_ready")
        work_read = sem("work_read")
        hi_ready = sem("hi_ready")
        xbo_ready = sem("xbo_ready")
        l0_scores = sem("l0_scores")
        l0_clipped = sem("l0_clipped")
        l0_exped = sem("l0_exped")
        l0_sums = sem("l0_sums")
        l0_ctx = sem("l0_ctx")
        l0_lned = sem("l0_lned")
        l0_inv = sem("l0_inv")
        l0_scaled = sem("l0_scaled")
        l0_summed = sem("l0_summed")
        l1_scores = sem("l1_scores")
        l1_masked = sem("l1_masked")
        l1_exped = sem("l1_exped")
        l1_turned = sem("l1_turned")
        l1_copied0 = sem("l1_copied0")
        l1_copied1 = sem("l1_copied1")
        l1_ctx = sem("l1_ctx")
        l1_recip = sem("l1_recip")
        l1_expanded = sem("l1_expanded")
        l1_normed = sem("l1_normed")
        stats_made = sem("stats_made")
        moments_made = sem("moments_made")
        ln_steps = sem("ln_steps")

        waits_passed = {e: sem(f"waits_passed_{e}") for e in ("sp", "dve", "pool")}

        def ln_base(m):
            return 1 + (11 * m.b if m.layer == 0 else 11 * B + 4 * m.b)

        def moments_base(m):
            return 2 * m.b if m.layer == 0 else 2 * B + m.b

        def use(m, prev, nxt, name):
            return m.at + uses_of(m, prev, nxt).index(name) + 1

        def on_dve(u):
            return u % 4 != 3

        def stack(eng, passed, m, which, first_use, slots=(0, 1, 2, 3)):
            dst = (q_stack if which == "Q" else k_stack)[m.par]
            done = q_stacked if which == "Q" else k_stacked if eng is nc.sync else first_k_stacked
            parts = (hi, hi, lo, lo) if which == "Q" else (hi, lo, hi, lo)
            wait_alone(eng, work_read, first_use + 1, passed)
            if m.layer == 0:
                wait_alone(eng, l0_scores, UNITS * (m.b - 1), passed)
            else:
                wait_alone(eng, l0_scores, UNITS * B - UNITS * (1 if m.first else 0), passed)
                wait_alone(eng, l1_scores, UNITS * (m.b - 1), passed)
            for j in slots:
                for h in range(HEADS):
                    eng.dma_start(dst[HD * j:HD * j + HD, h, :].bitcast(F32),
                                  parts[j][which][HD * h:HD * h + HD, :].bitcast(F32)).then_inc(done, DMA)

        def wait_stacked(eng, which, m, batches):
            if which == "Q":
                wait(eng, q_stacked, DMA * STACK_DMAS * (m.g + batches))
                return
            if isinstance(m.g, int) and m.g + batches == 1:
                eng.wait_ge(first_k_stacked, DMA * STACK_DMAS // 2)
            wait(eng, k_stacked, DMA * (STACK_DMAS * (m.g + batches) - STACK_DMAS // 2))

        def take_v(eng, m, half, n, bank):
            eng.wait_ge(work_ready, n)
            if m.layer == 0:
                wait(eng, l0_ctx, PAIRS * (m.b - 1))
            else:
                eng.wait_ge(l0_ctx, PAIRS * B - PAIRS * (1 if m.first else 0))
                wait(eng, l1_ctx, T * (m.b - 1))
            target = v_tok[m.par][:, 4 * half:4 * half + 4, :]
            values = bank.rearrange("p (t f) -> p t f", t=4)
            if eng is nc.scalar:
                eng.activation(target, values, ACT.Copy).then_inc(work_read, 1)
            elif m.layer == 0:
                eng.tensor_copy(target, values).then_inc(work_read, 1)
            else:
                eng.tensor_tensor(target, values, b_all[:, 3, :][:, None, :].to_broadcast([P, 4, P]), ALU.add)\
                   .then_inc(work_read, 1)

        def walk(eng, body, prologue, epilogue):
            def batch(layer, par, b, turn):
                if layer == 0:
                    at = FIRST_USES if isinstance(b, int) and b == 0 else FIRST_USES - 1 + 10 * b
                else:
                    first = isinstance(b, int) and b == 0
                    at = FIRST_USES + 10 * B - (1 if first else 2) + 12 * b
                return Batch(layer, par, b + B * layer, b, turn, isinstance(b, int) and b == 0, at)

            prologue(batch(0, 0, 0, 0))
            for layer in range(2):
                before = batch(0, 1, B - 1, B // 2 - 1) if layer else None
                body(batch(layer, 0, 0, 0), before, batch(layer, 1, 1, 0))
                with eng.Fori(0, (B - 2) // 2) as i:
                    odd, even = batch(layer, 1, 2 * i + 1, i), batch(layer, 0, 2 * i + 2, i + 1)
                    body(odd, batch(layer, 0, 2 * i, i), even)
                    body(even, odd, batch(layer, 1, 2 * i + 3, i + 1))
                last = batch(layer, 1, B - 1, B // 2 - 1)
                body(last, batch(layer, 0, B - 2, B // 2 - 1), batch(1, 0, 0, 0) if layer == 0 else None)
            epilogue(last)

        def setup_bank(i):
            return work[:, :] if i % 4 == 3 else acc[:, i % 4, :]

        def last_at():
            return FIRST_USES - 2 + 10 * B + 12 * (B - 1) + 4

        TAIL = range(UNITS, UNITS + 7)

        def at_once(m):
            return m.layer == 1 and m.first

        block = ctx.enter_context(nc.Block())

        @block.sync
        def _(sp):
            for half in stored:
                sp.sem_inc(half, DMA)
            w_in = x_t[:, :].rearrange("p (l m f) -> p l m f", l=2, m=4)
            for i, w in enumerate((wq0, wk0, wv0, wo0, wq1, wk1, wv1, wo1)):
                sp.dma_start(w_in[:, i // 4, i % 4, :], w).then_inc(weights_loaded, DMA)
            sp.dma_start(x_in[:, :, :], x_view[0]).then_inc(xin_loaded, DMA)
            adj_view = adj.rearrange("(t p) k -> p t k", p=P)
            adj_in = ring[:, :, :].bitcast(I32)
            for i, loaded in enumerate(adj_loaded):
                sp.dma_start(adj_in[:, 2 * i:2 * i + 2, :], adj_view[:, 2 * i:2 * i + 2, :]).then_inc(loaded, DMA)

            def store(m):
                target = x1_view if m.layer == 0 else out_view
                wait_alone(sp, ln_steps, ln_base(m) + (11 if m.layer == 0 else 4), waits_passed["sp"])
                sp.dma_start(one(target, m.b), y[m.par][:, :, :]).then_inc(stored[m.par], DMA)

            def body(m, prev, nxt):
                if nxt is not None:
                    wait_alone(sp, hi_ready, 4 * m.g + 4, waits_passed["sp"])
                    if nxt.layer == 1:
                        wait_alone(sp, stored[nxt.par], DMA * (nxt.turn + 2), waits_passed["sp"])
                    source = x_view if nxt.layer == 0 else x1_view
                    sp.dma_start(x_in[:, :, :], one(source, nxt.b)).then_inc(xin_loaded, DMA)
                    stack(sp, waits_passed["sp"], nxt, "Q", use(m, prev, nxt, "Q0"))
                    stack(sp, waits_passed["sp"], nxt, "K", use(m, prev, nxt, "K0"))
                if prev is not None:
                    store(prev)

            def prologue(m):
                stack(sp, waits_passed["sp"], m, "Q", 3)
                stack(sp, waits_passed["sp"], m, "K", 5, (0, 1))

            def epilogue(m):
                for half in range(2):
                    sp.wait_ge(ln_steps, ln_base(m) + 3 + half)
                    sp.dma_start(out_view[m.b, :, 4 * half:4 * half + 4, :],
                                 y[m.par][:, 4 * half:4 * half + 4, :]).then_inc(stored[m.par], DMA)
                sp.wait_ge(stored[0], DMA * (B + 1))
                sp.wait_ge(stored[1], DMA * (B + 2))

            walk(sp, body, prologue, epilogue)

        @block.tensor
        def _(pe):
            def fill(n):
                wait(pe, work_read, n - 1)

            def turn_tile(out, tile):
                return pe.transpose(out, tile, ident[:, :])

            def turn_weights(layer):
                for m in range(4):
                    mm = turn_tile(score[:, 0, layer * HALF + m * P:layer * HALF + (m + 1) * P],
                                   x_t[:, (layer * 4 + m) * P:(layer * 4 + m + 1) * P])
                mm.then_inc(weights_turned, 1)

            def spread_rows():
                pe.wait_ge(rows_loaded, DMA * 11)
                for i, (a, b) in enumerate(((0, 4), (4, 6))):
                    pe.matmul(score[:, 1, i * HALF:i * HALF + (b - a) * P], ones[0:1, :], b_rows[0:1, a * P:b * P],
                              start=True, stop=True).then_inc(weights_turned, 1)
                pe.wait_ge(bias_scaled, 2)
                pe.matmul(score[:, 0, 0:P], b_cols[:, 4:5].to_broadcast([P, P]), w_t[:, 0, 3, :],
                          start=True, stop=True).then_inc(weights_turned, 1)

            def prep(m, name, n, bank=work[:, :]):
                half = int(name[1])
                cols = slice(half * HALF, (half + 1) * HALF)
                if m.layer == 0 and m.first:
                    wait(pe, work_read, n - 4)
                else:
                    fill(n)
                if name[0] == "X":
                    if half == 0:
                        pe.wait_ge(xin_loaded, DMA * (m.g + 1))
                    for t in range(4):
                        mm = turn_tile(bank[:, t * P:(t + 1) * P], x_in[:, 4 * half + t, :])
                elif name[0] == "V":
                    for t in range(4):
                        mm = pe.matmul(bank[:, t * P:(t + 1) * P], x_t[:, (4 * half + t) * P:(4 * half + t + 1) * P],
                                       w_t[:, m.layer, 2, :], start=True, stop=True)
                else:
                    mm = pe.matmul(bank, w_t[:, m.layer, "QK".index(name[0]), :], x_t[:, cols],
                                   start=True, stop=True)
                mm.then_inc(work_ready, 1)

            def project(m, half, n):
                fill(n)
                if m.layer == 0:
                    pe.wait_ge(l0_summed, 14 * m.b + 7 * (half + 1))
                else:
                    pe.wait_ge(l1_normed, 2 * m.b + half + 1)
                for t in range(4):
                    mm = pe.matmul(work[:, t * P:(t + 1) * P], ctx_t[:, half, t * P:(t + 1) * P],
                                   w_t[:, m.layer, 3, :], start=True, stop=True)
                mm.then_inc(work_ready, 1)

            def turn_inverse(m, half, n):
                fill(n)
                pe.wait_ge(l1_expanded, 2 * m.b + half + 1)
                for t in range(4):
                    mm = turn_tile(work[:, t * P:(t + 1) * P], norm_row[:, 0, t * P:(t + 1) * P])
                mm.then_inc(work_ready, 1)

            def scores(m, u):
                if u == 0:
                    wait_stacked(pe, "Q", m, 1)
                    wait_stacked(pe, "K", m, 1)
                    if m.layer == 0 and m.first:
                        for clipped in mask_clipped:
                            pe.wait_ge(clipped, T // 2)
                    if m.layer == 1 and m.first:
                        pe.wait_ge(l0_clipped, UNITS * B)
                qs, ks = q_stack[m.par], k_stack[m.par]
                if m.layer == 0:
                    wait(pe, l0_clipped, UNITS * m.b + u - 1)
                    half, kt, hp = u // 16, u // 2 % 8, u % 2
                    for i in range(2):
                        h = 2 * hp + i
                        mm = pe.matmul(score[:, u % 2, i * HALF:(i + 1) * HALF], ks[:, h, kt * P:(kt + 1) * P],
                                       qs[:, h, half * HALF:(half + 1) * HALF], start=True, stop=True)
                    mm.then_inc(l0_scores, 1)
                else:
                    wait(pe, l1_masked, UNITS * m.b + u - 1)
                    qt, h = u // 4, u % 4
                    for i in range(2):
                        mm = pe.matmul(score[:, u % 2, i * HALF:(i + 1) * HALF], qs[:, h, qt * P:(qt + 1) * P],
                                       ks[:, h, i * HALF:(i + 1) * HALF], start=True, stop=True)
                    mm.then_inc(l1_scores, 1)

            def pair(m, p):
                pe.wait_ge(l0_exped, UNITS * m.b + 2 * p + 2)
                for what in range(2):
                    if (what == 0) == (p == 0):
                        wait(pe, l0_lned, PAIRS * m.b + p)
                    else:
                        wait(pe, l0_scaled, PAIRS * m.b + (p - 1 if p else 0))
                    bank = (2 * p + what) % 3
                    for h in range(HEADS):
                        u = 2 * p + h // 2
                        w = v_tok[m.par][:, p % 8, HD * h:HD * h + HD] if what else ones[:, 0:HD]
                        mm = pe.matmul(acc[HD * h:HD * h + HD, bank, :], w,
                                       ring[:, u % RING, (h % 2) * HALF:(h % 2 + 1) * HALF],
                                       start=True, stop=True)
                    mm.then_inc(l0_ctx if what else l0_sums, 1)

            def turn(m, u):
                pe.wait_ge(l1_exped, UNITS * m.b + u + 1)
                if m.first and u == 0:
                    pe.wait_ge(l0_lned, PAIRS * B)
                    pe.wait_ge(l0_scaled, PAIRS * B)
                for c in range(2):
                    wait(pe, (l1_copied0, l1_copied1)[c], UNITS * m.b + u)
                    for t in range(4):
                        mm = turn_tile(acc[:, c, t * P:(t + 1) * P],
                                       stage[:, u % STAGE, (4 * c + t) * P:(4 * c + t + 1) * P])
                    mm.then_inc(l1_turned, 1)

            def context(m, qt, part):
                if part == 0:
                    pe.wait_ge(l1_copied0, UNITS * m.b + 4 * qt + 4)
                    pe.wait_ge(l1_copied1, UNITS * m.b + 4 * qt + 4)
                    if qt % 4 == 0:
                        wait(pe, l1_normed, 2 * m.b + qt // 4)
                for kt in ((0, 1, 2), (3, 4), (5, 6, 7))[part]:
                    for h in range(HEADS):
                        mm = pe.matmul(acc[HD * h:HD * h + HD, 2, (qt % 4) * P:(qt % 4 + 1) * P],
                                       v_tok[m.par][:, kt, HD * h:HD * h + HD],
                                       ring[:, (4 * qt + h) % RING, kt * P:(kt + 1) * P],
                                       start=(kt == 0), stop=(kt == T - 1))
                if part == 2:
                    mm.then_inc(l1_ctx, 1)

            def attend(m, s):
                if m.layer == 0:
                    if s % 2 and 5 <= s <= 35:
                        pair(m, (s - 5) // 2)
                else:
                    if 3 <= s < UNITS + 3:
                        turn(m, s - 3)
                    if 7 <= s < UNITS + 6 and (s - 7) % 4 < 3:
                        context(m, (s - 7) // 4, (s - 7) % 4)

            PREP_AT = {10: "X0", 11: "X1", 12: "Q0", 14: "Q1", 16: "K0", 18: "K1", 22: "V0", 24: "V1"}

            def body(m, prev, nxt):
                if at_once(m):
                    for s in TAIL:
                        attend(prev, s)
                for s in range(UNITS):
                    scores(m, s)
                    if prev is not None:
                        if not at_once(m):
                            attend(prev, s + UNITS)
                        if prev.layer and s == 5:
                            turn_inverse(prev, 1, use(m, prev, nxt, "R1"))
                        if s == 8:
                            project(prev, 1, use(m, prev, nxt, "Wo1"))
                    attend(m, s)
                    if nxt is not None and s in PREP_AT:
                        prep(nxt, PREP_AT[s], use(m, prev, nxt, PREP_AT[s]))
                    if m.layer and s == 20:
                        turn_inverse(m, 0, use(m, prev, nxt, "R0"))
                    if s == 28:
                        project(m, 0, use(m, prev, nxt, "Wo0"))

            def prologue(m):
                pe.wait_ge(consts_made, 5)
                pe.wait_ge(weights_loaded, DMA * 8)
                turn_weights(0)
                turn_weights(1)
                for i, name in enumerate(("X0", "X1", "Q0", "Q1", "K0", "K1", "V0", "V1")):
                    if name == "Q0":
                        pe.wait_ge(weights_placed, 1)
                        pe.wait_ge(work_read, 2)
                    prep(m, name, i + 1, setup_bank(i))
                spread_rows()
                score_bf = score[:, :, :].bitcast(BF16).rearrange("p a (c n) -> p (a c) n", c=2)
                pe.wait_ge(mask_biased, T)
                pe.wait_ge(weights_placed, 5)
                for kt in range(T):
                    wait(pe, mask_clipped[kt % 2], kt // 2 - 1)
                    for qt in range(T):
                        mm = pe.transpose(score_bf[:, kt % 4, qt * P:(qt + 1) * P],
                                          bias_mask[:, qt, kt * P:(kt + 1) * P], ident_bf[:, :])
                    mm.then_inc(mask_turned, 1)

            def epilogue(m):
                for s in range(UNITS, UNITS + 5):
                    attend(m, s)
                turn_inverse(m, 1, last_at() + 1)
                attend(m, UNITS + 5)
                project(m, 1, last_at() + 2)

            walk(pe, body, prologue, epilogue)

        @block.vector
        def _(dve):
            def place_weights(layer):
                dve.wait_ge(weights_turned, layer + 1)
                turned = score[:, 0, layer * HALF:(layer + 1) * HALF]
                dve.tensor_scalar(w_t[:, layer, 0, :], turned[:, 0:P], SCALE, None, ALU.mult)
                dve.tensor_copy(w_t[:, layer, 1:4, :],
                                turned[:, P:4 * P].rearrange("p (m f) -> p m f", m=3)).then_inc(weights_placed, 1)

            def place_rows():
                for i, (a, b) in enumerate(((0, 4), (4, 6))):
                    dve.wait_ge(weights_turned, 3 + i)
                    dve.tensor_copy(b_all[:, a:b, :],
                                    score[:, 1, i * HALF:i * HALF + (b - a) * P].rearrange("p (m f) -> p m f", f=P))\
                       .then_inc(weights_placed, 1)
                dve.wait_ge(weights_turned, 5)
                dve.wait_ge(weights_placed, 4)
                dve.tensor_tensor(b_all[:, 0, :], score[:, 0, 0:P], b_all[:, 0, :], ALU.add)\
                   .then_inc(weights_placed, 1)

            adj_in = ring[:, :, :].bitcast(I32)
            score_bf = score[:, :, :].bitcast(BF16).rearrange("p a (c n) -> p (a c) n", c=2)

            def bias_masks():
                for t in range(T):
                    if t % 2 == 0:
                        dve.wait_ge(adj_loaded[t // 2], DMA)
                    dve.tensor_scalar(bias_mask[:, t, :], adj_in[:, t, :], 0.0, MASKED, ALU.is_equal, ALU.mult)\
                       .then_inc(mask_biased, 1)

            def clip_masks():
                for kt in range(0, T, 2):
                    dve.wait_ge(mask_turned, kt + 1)
                    dve.tensor_scalar(clip_mask[:, kt, :], score_bf[:, kt % 4, :], -2 * CLIP, CLIP,
                                      ALU.max, ALU.add).then_inc(mask_clipped[0], 1)

            def low_part(m, name, n, bank=work[:, :]):
                which, half = name[0], int(name[1])
                cols = slice(half * HALF, (half + 1) * HALF)
                k = ("Q0", "Q1", "K0", "K1").index(name)
                dve.wait_ge(hi_ready, 4 * m.g + k + 1)
                c = 2 * m.layer + "QK".index(which)
                dve.scalar_tensor_tensor(out=lo[which][:, cols], in0=bank, scalar=b_cols[:, c:c + 1],
                                         in1=hi[which][:, cols].bitcast(F32), op0=ALU.add, op1=ALU.subtract)\
                   .then_inc(work_read, 1)

            def clip(m, u):
                dve.wait_ge(l0_scores, UNITS * m.b + u + 1)
                wait(dve, l0_exped, UNITS * m.b + u - STAGE + 1)
                half, kt = u // 16, u // 2 % 8
                dve.scalar_tensor_tensor(
                    out=stage[:, u % STAGE, :].rearrange("p (h n) -> p h n", h=2),
                    in0=score[:, u % 2, :].rearrange("p (h n) -> p h n", h=2), scalar=-CLIP,
                    in1=clip_mask[:, kt, half * HALF:(half + 1) * HALF][:, None, :].to_broadcast([P, 2, HALF]),
                    op0=ALU.max, op1=ALU.min).then_inc(l0_clipped, 1)

            def scale_pair(m, p):
                dve.wait_ge(l0_ctx, PAIRS * m.b + p + 1)
                dve.wait_ge(l0_inv, PAIRS * m.b + p + 1)
                half, kt = p // 8, p % 8
                if kt == 0:
                    target = ctx_t[:, half, :]
                else:
                    target = scaled[:, p % 2, :]
                    adds = 7 * half + kt - 1
                    wait(dve, l0_summed, 14 * m.b + adds - (1 if kt > 1 else 0))
                dve.tensor_tensor(target, acc[:, (2 * p + 1) % 3, :], norm_row[:, p % 2, :], ALU.mult)\
                   .then_inc(l0_scaled, 1)

            def mask_max(m, u):
                dve.wait_ge(l1_scores, UNITS * m.b + u + 1)
                wait_alone(dve, l1_turned, 2 * (UNITS * m.b + u - STAGE + 1), waits_passed["dve"])
                if m.first and u == 0:
                    dve.wait_ge(l0_exped, UNITS * B)
                dve.tensor_tensor_reduce(
                    out=stage[:, u % STAGE, :], in0=score[:, u % 2, :], in1=bias_mask[:, u // 4, :],
                    scale=-1.0, scalar=3e38, op0=ALU.add, op1=ALU.min,
                    accum_out=row_max[:, m.par, u:u + 1]).then_inc(l1_masked, 1)

            def copy_turned(m, u):
                dve.wait_ge(l1_turned, 2 * (UNITS * m.b + u + 1))
                wait(dve, l1_ctx, T * m.b + u // 4 - 1)
                dve.tensor_copy(ring[:, u % RING, HALF:N], acc[:, 1, :]).then_inc(l1_copied1, 1)

            def invert(m, half):
                dve.wait_ge(l1_exped, UNITS * m.b + 16 * (half + 1))
                wait(dve, l1_expanded, 2 * m.b + half)
                units = slice(16 * half, 16 * half + 16)
                dve.reciprocal(inv_sum[:, :], row_sum[:, m.par, units]).then_inc(l1_recip, 1)
                dve.wait_ge(l1_recip, 4 * m.b + 2 * half + 1)
                dve.scalar_tensor_tensor(out=inv_sum[:, :], in0=row_max[:, m.par, units], scalar=-0.5 * MASKED,
                                         in1=inv_sum[:, :], op0=ALU.is_lt, op1=ALU.mult).then_inc(l1_recip, 1)

            def normalise(m, half, n):
                dve.wait_ge(l1_ctx, T * m.b + 4 * (half + 1))
                dve.wait_ge(work_read, n)
                dve.tensor_tensor(ctx_t[:, half, :], acc[:, 2, :], norm_row[:, 1, :], ALU.mult).then_inc(l1_normed, 1)

            def add_residual(m, half, n):
                dve.wait_ge(work_ready, n)
                if half == 0:
                    dve.wait_ge(xbo_ready, m.g + 1)
                    wait(dve, stored[m.par], DMA * (m.turn + B // 2 * m.layer + 1))
                dve.tensor_tensor(y[m.par][:, 4 * half:4 * half + 4, :],
                                  work[:, :].rearrange("p (t f) -> p t f", t=4),
                                  x_bo[:, 4 * half:4 * half + 4, :], ALU.add).then_inc(work_read, 1)

            def layer_stats(m, which, n, part):
                if which == 0 and part == 0:
                    dve.wait_ge(work_read, n)
                    wait(dve, ln_steps, ln_base(m))
                elif part == 0:
                    dve.wait_ge(ln_steps, ln_base(m) + 7)
                for t in (2 * part, 2 * part + 1):
                    dve.bn_stats(stats[:, t, :], y[m.par][:, t, :]).then_inc(stats_made, 1)
                if part == 3:
                    wait_alone(dve, stats_made, T * (moments_base(m) + which + 1), waits_passed["dve"])
                    for t in range(T):
                        mm = dve.bn_aggr(moments[:, t, :], stats[:, t, :])
                    mm.then_inc(moments_made, 1)

            def attend(m, s):
                if m.layer == 0:
                    if s % 2 == 0 and 6 <= s <= 36:
                        scale_pair(m, (s - 6) // 2)
                else:
                    if 2 <= s < UNITS + 2 and on_dve(s - 2):
                        copy_turned(m, s - 2)

            LOW_AT = {12: "Q0", 14: "Q1", 16: "K0", 18: "K1"}
            V_AT = {22: 0, 24: 1}

            def body(m, prev, nxt):
                if at_once(m):
                    for s in TAIL:
                        attend(prev, s)
                for s in range(UNITS):
                    (mask_max if m.layer else clip)(m, s)
                    if prev is not None:
                        if not at_once(m):
                            attend(prev, s + UNITS)
                        if prev.layer and s == 1:
                            invert(prev, 1)
                        if prev.layer and s == 5:
                            normalise(prev, 1, use(m, prev, nxt, "R1"))
                        if s == 8:
                            add_residual(prev, 1, use(m, prev, nxt, "Wo1"))
                        if 9 <= s < 13:
                            layer_stats(prev, 0, use(m, prev, nxt, "Wo1"), s - 9)
                        if prev.layer == 0 and 22 <= s < 26:
                            layer_stats(prev, 1, None, s - 22)
                    if nxt is not None:
                        if s in LOW_AT:
                            low_part(nxt, LOW_AT[s], use(m, prev, nxt, LOW_AT[s]))
                        if s in V_AT and nxt.layer == 1:
                            take_v(dve, nxt, V_AT[s], use(m, prev, nxt, f"V{V_AT[s]}"), work[:, :])
                    if m.layer and s == 17:
                        invert(m, 0)
                    if m.layer and s == 21:
                        normalise(m, 0, use(m, prev, nxt, "R0"))
                    if s == 28:
                        add_residual(m, 0, use(m, prev, nxt, "Wo0"))
                    attend(m, s)

            def prologue(m):
                place_weights(0)
                dve.wait_ge(rows_loaded, DMA * 11)
                dve.tensor_scalar(b_cols[:, 0:4:2], b_cols[:, 0:4:2], SCALE, None, ALU.mult).then_inc(bias_scaled, 1)
                dve.tensor_scalar(b_cols[:, 4:5], b_cols[:, 4:5], float(T), None, ALU.mult).then_inc(bias_scaled, 1)
                place_weights(1)
                for i, name in enumerate(("Q0", "Q1", "K0", "K1")):
                    low_part(m, name, 3 + i, setup_bank(2 + i))
                bias_masks()
                place_rows()
                for half in range(2):
                    take_v(dve, m, half, 7 + half, setup_bank(6 + half))
                clip_masks()

            def epilogue(m):
                for s in range(UNITS, UNITS + 2):
                    attend(m, s)
                invert(m, 1)
                normalise(m, 1, last_at() + 1)
                add_residual(m, 1, last_at() + 2)
                for part in range(4):
                    layer_stats(m, 0, last_at() + 2, part)
                dve.wait_ge(ln_steps, ln_base(m) + 2)
                for t in range(T):
                    mm = dve.tensor_scalar(y[m.par][:, t, :], y[m.par][:, t, :], moments[:, t, 0:1], rstd[:, t:t + 1],
                                           ALU.subtract, ALU.mult)
                    if t % 4 == 3:
                        mm.then_inc(ln_steps, 1)

            walk(dve, body, prologue, epilogue)

        @block.scalar
        def _(act):
            for i, v in enumerate((bq0, bk0, bq1, bk1, bv0)):
                act.dma_start(b_cols[:, i:i + 1], v.rearrange("(d a) -> d a", a=1)).then_inc(rows_loaded, DMA)
            for i, v in enumerate((bo0, bo1, bv0, bv1, gamma, beta)):
                act.dma_start(b_rows[0:1, i * P:(i + 1) * P], v.rearrange("(a d) -> a d", a=1))\
                   .then_inc(rows_loaded, DMA)
            act.preload_act_table_set("natural_log_exp_and_others")

            def take_x(half, n, bank=work[:, :]):
                act.wait_ge(work_ready, n)
                act.activation(x_t[:, half * HALF:(half + 1) * HALF], bank, ACT.Copy).then_inc(work_read, 1)

            def high_part(m, name, n, bank=work[:, :]):
                which, half = name[0], int(name[1])
                act.wait_ge(work_ready, n)
                wait_stacked(act, which, m, 0)
                c = 2 * m.layer + "QK".index(which)
                act.activation(hi[which][:, half * HALF:(half + 1) * HALF], bank, ACT.Identity,
                               bias=b_cols[:, c:c + 1]).then_inc(hi_ready, 1)

            def exp0(m, u):
                act.wait_ge(l0_clipped, UNITS * m.b + u + 1)
                wait(act, l0_ctx, PAIRS * m.b + u // 2 - 3)
                act.activation(ring[:, u % RING, :], stage[:, u % STAGE, :], ACT.Exp).then_inc(l0_exped, 1)

            def log_sums(m, p):
                act.wait_ge(l0_sums, PAIRS * m.b + p + 1)
                wait(act, l0_scaled, PAIRS * m.b + p - 1)
                act.activation(norm_row[:, p % 2, :], acc[:, (2 * p) % 3, :], ACT.Ln).then_inc(l0_lned, 1)

            def inverse_sums(m, p):
                act.wait_ge(l0_lned, PAIRS * m.b + p + 1)
                act.activation(norm_row[:, p % 2, :], norm_row[:, p % 2, :], ACT.Exp, scale=-1.0).then_inc(l0_inv, 1)

            def exp1(m, u):
                act.wait_ge(l1_masked, UNITS * m.b + u + 1)
                act.activation(stage[:, u % STAGE, :], stage[:, u % STAGE, :], ACT.Exp,
                               bias=row_max[:, m.par, u:u + 1], scale=-1.0,
                               accum_out=row_sum[:, m.par, u:u + 1]).then_inc(l1_exped, 1)

            def copy_turned(m, u, c):
                act.wait_ge(l1_turned, 2 * (UNITS * m.b + u) + c + 1)
                wait(act, l1_ctx, T * m.b + u // 4 - 1)
                act.activation(ring[:, u % RING, c * HALF:(c + 1) * HALF], acc[:, c, :], ACT.Copy)\
                   .then_inc((l1_copied0, l1_copied1)[c], 1)

            def take_inverse(m, half, n):
                act.wait_ge(work_ready, n)
                wait(act, l1_normed, 2 * m.b + half)
                act.activation(norm_row[:, 1, :], work[:, :], ACT.Copy).then_inc(work_read, 1)

            def attend(m, s):
                if m.layer == 1 and 1 <= s < UNITS + 1:
                    copy_turned(m, s - 1, 0)
                    if not on_dve(s - 1):
                        copy_turned(m, s - 1, 1)

            def pair_before(m, s):
                if m is not None and m.layer == 0 and s % 2 == 0 and 4 <= s <= 34:
                    log_sums(m, (s - 4) // 2)

            def pair_after(m, s):
                if m is not None and m.layer == 0 and s % 2 == 0 and 4 <= s <= 34:
                    inverse_sums(m, (s - 4) // 2)

            def body(m, prev, nxt):
                if at_once(m):
                    for s in TAIL:
                        pair_before(prev, s)
                        pair_after(prev, s)
                for s in range(UNITS):
                    if not at_once(m):
                        pair_before(prev, s + UNITS)
                    pair_before(m, s)
                    if prev is not None and prev.layer and s == 4:
                        take_inverse(prev, 1, use(m, prev, nxt, "R1"))
                    if nxt is not None:
                        if s in (9, 10):
                            take_x(s - 9, use(m, prev, nxt, f"X{s - 9}"))
                        if s in (11, 13, 15, 17):
                            name = {11: "Q0", 13: "Q1", 15: "K0", 17: "K1"}[s]
                            high_part(nxt, name, use(m, prev, nxt, name))
                        if s in (21, 23) and nxt.layer == 0:
                            half = (s - 21) // 2
                            take_v(act, nxt, half, use(m, prev, nxt, f"V{half}"), work[:, :])
                    if m.layer and s == 19:
                        take_inverse(m, 0, use(m, prev, nxt, "R0"))
                    (exp1 if m.layer else exp0)(m, s)
                    if not at_once(m):
                        pair_after(prev, s + UNITS)
                    pair_after(m, s)
                    if prev is not None:
                        attend(prev, s + UNITS)
                    attend(m, s)

            def prologue(m):
                act.wait_ge(weights_turned, 2)
                for half in range(2):
                    take_x(half, 1 + half, setup_bank(half))
                act.wait_ge(bias_scaled, 1)
                for i, name in enumerate(("Q0", "Q1", "K0", "K1")):
                    high_part(m, name, 3 + i, setup_bank(2 + i))
                score_bf = score[:, :, :].bitcast(BF16).rearrange("p a (c n) -> p (a c) n", c=2)
                for kt in range(1, T, 2):
                    act.wait_ge(mask_turned, kt + 1)
                    act.activation(clip_mask[:, kt, :], score_bf[:, kt % 4, :], ACT.Copy,
                                   scale=2 * CLIP / -MASKED, bias=CLIP).then_inc(mask_clipped[1], 1)
                act.wait_ge(mask_biased, T)

            def epilogue(m):
                attend(m, UNITS)
                take_inverse(m, 1, last_at() + 1)

            walk(act, body, prologue, epilogue)

        @block.gpsimd
        def _(pool):
            pool.memset(ident[:, :], 0.0).then_inc(consts_made, 1)
            pool.memset(ones[:, :], 1.0).then_inc(consts_made, 1)
            pool.memset(power[:, :], -0.5).then_inc(consts_made, 1)
            pool.wait_ge(consts_made, 3)
            pool.affine_select(out=ident[:, :], in_=ident[:, :], compare_op=ALU.not_equal, fill=1.0, base=0,
                               pattern=[[-1, P]], channel_multiplier=1).then_inc(consts_made, 1)
            pool.wait_ge(consts_made, 4)
            pool.tensor_copy(ident_bf[:, :], ident[:, :]).then_inc(consts_made, 1)
            pool.sem_inc(ln_steps, 1)

            def spread(row):
                return row[:, None, :].to_broadcast([P, T, P])

            def per_token(col):
                return col[:, :, None].to_broadcast([P, T, P])

            def load_residual(m, prev):
                if m.layer == 1:
                    wait_alone(pool, stored[m.par], DMA * (m.turn + 2), waits_passed["pool"])
                source = x_view if m.layer == 0 else x1_view
                if prev is not None:
                    wait_alone(pool, xbo_ready, m.g, waits_passed["pool"])
                    if prev.layer == 0:
                        wait_alone(pool, ln_steps, ln_base(prev) + 7, waits_passed["pool"])
                pool.dma_start(x_res[:, :, :], one(source, m.b)).then_inc(xres_loaded, DMA)

            def add_bias(m, prev, n_free):
                pool.wait_ge(xres_loaded, DMA * (m.g + 1))
                if prev is not None:
                    pool.wait_ge(work_read, n_free)
                else:
                    pool.wait_ge(weights_placed, 5)
                pool.tensor_tensor(x_bo[:, :, :], x_res[:, :, :], spread(b_all[:, m.layer, :]), ALU.add)\
                    .then_inc(xbo_ready, 1)

            def step(op, m, k):
                if k > 1:
                    wait_alone(pool, ln_steps, ln_base(m) + k - 1, waits_passed["pool"])
                op().then_inc(ln_steps, 1)

            def normalise_tokens(m, k):
                which, k0 = (0, 0) if k < 8 else (1, 7)
                if k == k0 + 1:
                    wait_alone(pool, moments_made, moments_base(m) + which + 1, waits_passed["pool"])
                yt = y[m.par][:, :, :]
                if k == k0 + 1:
                    step(lambda: pool.tensor_scalar(rstd[:, :], moments[:, :, 1], EPS, 1.0, ALU.add, ALU.mult), m, k)
                elif k == k0 + 2:
                    step(lambda: pool.tensor_tensor(rstd[:, :], rstd[:, :], power[:, :], ALU.pow), m, k)
                elif k == k0 + 3:
                    step(lambda: pool.tensor_tensor(yt, yt, per_token(moments[:, :, 0]), ALU.subtract), m, k)
                elif k == k0 + 4:
                    step(lambda: pool.tensor_tensor(yt, yt, per_token(rstd[:, :]), ALU.mult), m, k)

            def affine_residual(m, k):
                yt = y[m.par][:, :, :]
                other = {5: spread(b_all[:, 4, :]), 6: spread(b_all[:, 5, :]), 7: x_res[:, :, :]}[k]
                step(lambda: pool.tensor_tensor(yt, yt, other, ALU.mult if k == 5 else ALU.add), m, k)

            def sum_pair(m, p):
                half, kt = p // 8, p % 8
                pool.wait_ge(l0_scaled, PAIRS * m.b + p + 1)
                if kt:
                    wait(pool, l0_summed, 14 * m.b + 7 * half + kt - 1)
                    pool.tensor_tensor(ctx_t[:, half, :], ctx_t[:, half, :], scaled[:, p % 2, :], ALU.add)\
                        .then_inc(l0_summed, 1)

            def expand(m, half, n_free):
                pool.wait_ge(l1_recip, 4 * m.b + 2 * half + 2)
                if m.first and half == 0:
                    pool.wait_ge(l0_scaled, PAIRS * B)
                elif n_free is not None:
                    pool.wait_ge(work_ready, n_free)
                pool.tensor_tensor(norm_row[:, 0, :].rearrange("p (u d) -> p u d", d=HD),
                                   inv_sum[:, :, None].to_broadcast([P, 16, HD]),
                                   ones[:, 0:1][:, :, None].to_broadcast([P, 16, HD]), ALU.mult)\
                    .then_inc(l1_expanded, 1)

            def attend(m, s):
                if m.layer == 0 and s % 2 == 0 and 8 <= s <= 38:
                    sum_pair(m, (s - 8) // 2)

            LN_AT = ({13: (1, 2, 3), 15: (4,), 17: (5,), 19: (6,), 21: (7,), 27: (8, 9, 10), 29: (11,)},
                     {13: (1, 2, 3), 15: (4,)})

            def body(m, prev, nxt):
                if at_once(m):
                    for s in TAIL:
                        attend(prev, s)
                for s in range(UNITS):
                    if prev is not None:
                        if not at_once(m):
                            attend(prev, s + UNITS)
                        if prev.layer and s == 2:
                            r0 = prev.at + uses_of(prev, prev, m).index("R0") + (0 if prev.first else 1)
                            expand(prev, 1, r0)
                    attend(m, s)
                    if prev is not None:
                        for k in LN_AT[prev.layer].get(s, ()):
                            (affine_residual if 5 <= k <= 7 else normalise_tokens)(prev, k)
                    if s == 22:
                        load_residual(m, prev)
                    if m.layer and s == 18:
                        expand(m, 0, use(m, prev, nxt, "R1") if prev.layer else None)
                    if s == 25:
                        add_bias(m, prev, use(m, prev, nxt, "Wo1") if prev is not None else None)

            def prologue(m):
                stack(pool, waits_passed["pool"], m, "K", 5, (2, 3))

            def epilogue(m):
                expand(m, 1, m.at + 3)
                for k in (1, 2):
                    normalise_tokens(m, k)

            walk(pool, body, prologue, epilogue)


_INS = ["x", "adj"] + [f"L0_gnn_{n}" for n in ("Wq", "bq", "Wk", "bk", "Wv", "bv", "Wo", "bo", "gamma", "beta")] \
    + [f"L1_gnn_{n}" for n in ("wq", "bq", "wk", "bk", "wv", "bv", "wo", "bo")]


def kernel(**inputs):
    import numpy as _np
    import concourse.bacc as _bacc
    from concourse import mybir as _mybir
    from concourse.bass_utils import run_bass_kernel_spmd as _run

    nc = _bacc.Bacc("TRN2", target_bir_lowering=False, num_devices=1)
    arrays, args = {}, []
    for name in _INS:
        a = _np.ascontiguousarray(inputs[name])
        arrays[f"in_{name}"] = a
        args.append(nc.dram_tensor(f"in_{name}", a.shape, _mybir.dt.from_np(a.dtype), kind="ExternalInput").ap())
    shape = tuple(inputs["x"].shape)
    out = nc.dram_tensor("out_0", shape, _mybir.dt.float32, kind="ExternalOutput").ap()
    x1 = nc.dram_tensor("x1_scratch", shape, _mybir.dt.float32, kind="Internal").ap()
    adj_block_kernel(nc, *args, out, x1)
    r = _run(nc, [arrays], core_ids=[0])
    return r.results[0]["out_0"]
```
